# Optimizing a Trainium2 kernel written in Bass

```python
import numpy as np
import jax
import jax.numpy as jnp

def _softmax(x, axis=-1):
    return jax.nn.softmax(x, axis=axis)

def _gelu(x):
    return jax.nn.gelu(x, approximate=True)

def _silu(x):
    return jax.nn.silu(x)

def _sigmoid(x):
    return jax.nn.sigmoid(x)

def _layernorm(x, axis=-1, eps=1e-05):
    m = jnp.mean(x, axis=axis, keepdims=True)
    v = jnp.var(x, axis=axis, keepdims=True)
    return (x - m) / jnp.sqrt(v + eps)

def _scatter_add(tgt, idx, src, axis=0):
    return tgt.at[idx].add(src)

def _segment_sum(src, seg, n):
    return jax.ops.segment_sum(src, seg, n)
kernel_name = 'mk_conv_seq_d2_conv_nchw512_r4_e050a8'

def setup_inputs(seed: int=0):
    np.random.seed(seed)
    _w = jnp.asarray

    def _rec_inputs():
        import jax
        import jax.numpy as jnp
        _gk = jax.random.key(seed)
        x = -0.000929 + 1 * jax.random.normal(jax.random.fold_in(_gk, 1), (2, 128, 32, 32), jnp.float32)
        return x
    x = _rec_inputs()

    def _L0_conv_setup():
        import jax, jax.numpy as jnp
        import numpy as np
        B, C, H, W = (2, 128, 32, 32)
        HEADS = 8
        GROUPS = 8
        DH = 16
        DF = 4
        OFF_SCALE = 4.0
        EPS = 1e-05

        def _bn(t, gamma, beta):
            s = gamma / jnp.sqrt(1.0 + EPS)
            return t * s[None, :, None, None] + beta[None, :, None, None]

        def _gconv1x1(t, w):
            b, c, h, ww = t.shape
            o = jnp.einsum('bgci,goc->bgoi', t.reshape(b, GROUPS, c // GROUPS, h * ww), w)
            return o.reshape(b, GROUPS * w.shape[1], h, ww)

        def _grid_sample(img, grid):
            N, Ci, Hi, Wi = img.shape
            gx = (grid[..., 0] + 1.0) * (Wi / 2.0) - 0.5
            gy = (grid[..., 1] + 1.0) * (Hi / 2.0) - 0.5
            x0 = jnp.floor(gx)
            y0 = jnp.floor(gy)
            wx = gx - x0
            wy = gy - y0

            def gather(im, ix, iy):
                valid = (ix >= 0) & (ix < Wi) & (iy >= 0) & (iy < Hi)
                ixc = jnp.clip(ix, 0, Wi - 1).astype(jnp.int32)
                iyc = jnp.clip(iy, 0, Hi - 1).astype(jnp.int32)
                return im[:, iyc, ixc] * valid[None].astype(im.dtype)

            def sample_one(im, x0, y0, wx, wy):
                v00 = gather(im, x0, y0)
                v01 = gather(im, x0 + 1, y0)
                v10 = gather(im, x0, y0 + 1)
                v11 = gather(im, x0 + 1, y0 + 1)
                wx = wx[None]
                wy = wy[None]
                return v00 * (1 - wx) * (1 - wy) + v01 * wx * (1 - wy) + v10 * (1 - wx) * wy + v11 * wx * wy
            return jax.vmap(sample_one)(img, x0, y0, wx, wy)

        def _forward(x, bn1_g, bn1_b, bn2_g, bn2_b, qw, kw, vw, out_w, out_b, off_dw_w, off_dw_b, off_pw_w, cpb_w1, cpb_b1, cpb_w2, cpb_b2, cpb_w3, cpb_b3, mlp_w1, mlp_b1, mlp_w2, mlp_b2):
            b = x.shape[0]
            xn = _bn(x, bn1_g, bn1_b)
            q = _gconv1x1(xn, qw)
            qg = q.reshape(b * GROUPS, DH, H, W)
            off = jax.lax.conv_general_dilated(qg, off_dw_w, (DF, DF), ((1, 1), (1, 1)), dimension_numbers=('NCHW', 'OIHW', 'NCHW'), feature_group_count=DH)
            off = jax.nn.gelu(off + off_dw_b[None, :, None, None], approximate=False)
            off = jnp.tanh(jnp.einsum('bchw,oc->bohw', off, off_pw_w)) * OFF_SCALE
            Hd, Wd = (off.shape[-2], off.shape[-1])
            gy, gx = jnp.meshgrid(jnp.arange(Hd, dtype=x.dtype), jnp.arange(Wd, dtype=x.dtype), indexing='ij')
            vx = gx[None] + off[:, 0]
            vy = gy[None] + off[:, 1]
            nx = 2.0 * vx / max(Hd - 1, 1) - 1.0
            ny = 2.0 * vy / max(Wd - 1, 1) - 1.0
            vgrid_scaled = jnp.stack((nx, ny), axis=-1)
            kv = _grid_sample(xn.reshape(b * GROUPS, DH, H, W), vgrid_scaled)
            kv = kv.reshape(b, GROUPS * DH, Hd, Wd)
            k = _gconv1x1(kv, kw)
            v = _gconv1x1(kv, vw)
            scale = DH ** (-0.5)
            qh = q.reshape(b, HEADS, DH, H * W).transpose(0, 1, 3, 2) * scale
            kh = k.reshape(b, HEADS, DH, Hd * Wd).transpose(0, 1, 3, 2)
            vh = v.reshape(b, HEADS, DH, Hd * Wd).transpose(0, 1, 3, 2)
            qgy, qgx = jnp.meshgrid(jnp.arange(H, dtype=x.dtype), jnp.arange(W, dtype=x.dtype), indexing='ij')
            grid_q = jnp.stack((2.0 * qgx / max(H - 1, 1) - 1.0, 2.0 * qgy / max(W - 1, 1) - 1.0), axis=-1).reshape(1, H * W, 2)
            grid_kv = vgrid_scaled.reshape(b * GROUPS, Hd * Wd, 2)
            pos = grid_q[:, :, None, :] - grid_kv[:, None, :, :]
            bias = jnp.sign(pos) * jnp.log1p(jnp.abs(pos))
            bias = jax.nn.relu(bias @ cpb_w1 + cpb_b1)
            bias = jax.nn.relu(bias @ cpb_w2 + cpb_b2)
            bias = (bias @ cpb_w3 + cpb_b3).reshape(b, GROUPS, H * W, Hd * Wd)
            sim = jnp.einsum('bhid,bhjd->bhij', qh, kh) + bias
            attn = jax.nn.softmax(sim, axis=-1)
            out = jnp.einsum('bhij,bhjd->bhid', attn, vh)
            out = out.transpose(0, 1, 3, 2).reshape(b, HEADS * DH, H, W)
            out = jnp.einsum('bchw,oc->bohw', out, out_w) + out_b[None, :, None, None]
            x = x + out
            xn2 = _bn(x, bn2_g, bn2_b)
            h1 = jax.nn.gelu(jnp.einsum('bchw,oc->bohw', xn2, mlp_w1) + mlp_b1[None, :, None, None], approximate=False)
            return x + jnp.einsum('bchw,oc->bohw', h1, mlp_w2) + mlp_b2[None, :, None, None]
        ks = jax.random.split(jax.random.key(seed), 16)
        w = lambda k, shape: jax.random.normal(k, shape, dtype=jnp.float32) * 0.02
        return {'x': jax.random.normal(ks[0], (B, C, H, W), dtype=jnp.float32), 'bn1_g': jnp.ones((C,), jnp.float32), 'bn1_b': jnp.zeros((C,), jnp.float32), 'bn2_g': jnp.ones((C,), jnp.float32), 'bn2_b': jnp.zeros((C,), jnp.float32), 'qw': w(ks[1], (GROUPS, DH, C // GROUPS)), 'kw': w(ks[2], (GROUPS, DH, C // GROUPS)), 'vw': w(ks[3], (GROUPS, DH, C // GROUPS)), 'out_w': w(ks[4], (C, HEADS * DH)), 'out_b': jnp.zeros((C,), jnp.float32), 'off_dw_w': w(ks[5], (DH, 1, 6, 6)), 'off_dw_b': jnp.zeros((DH,), jnp.float32), 'off_pw_w': w(ks[6], (2, DH)), 'cpb_w1': w(ks[7], (2, 32)), 'cpb_b1': jnp.zeros((32,), jnp.float32), 'cpb_w2': w(ks[8], (32, 32)), 'cpb_b2': jnp.zeros((32,), jnp.float32), 'cpb_w3': w(ks[9], (32, 1)), 'cpb_b3': jnp.zeros((1,), jnp.float32), 'mlp_w1': w(ks[10], (4 * C, C)), 'mlp_b1': jnp.zeros((4 * C,), jnp.float32), 'mlp_w2': w(ks[11], (C, 4 * C)), 'mlp_b2': jnp.zeros((C,), jnp.float32)}
    _L0_conv_all = _L0_conv_setup()
    _L0_conv_in = {k: v for k, v in _L0_conv_all.items() if k in ('bn1_g', 'bn1_b', 'bn2_g', 'bn2_b', 'qw', 'kw', 'vw', 'out_w', 'out_b', 'off_dw_w', 'off_dw_b', 'off_pw_w', 'cpb_w1', 'cpb_b1', 'cpb_w2', 'cpb_b2', 'cpb_w3', 'cpb_b3', 'mlp_w1', 'mlp_b1', 'mlp_w2', 'mlp_b2')}
    del _L0_conv_all

    def _L1_conv_setup():
        import jax, jax.numpy as jnp
        import numpy as np
        B, C, H, W = (2, 128, 32, 32)
        HEADS = 8
        GROUPS = 8
        DH = 16
        DF = 4
        OFF_SCALE = 4.0
        EPS = 1e-05

        def _bn(t, gamma, beta):
            s = gamma / jnp.sqrt(1.0 + EPS)
            return t * s[None, :, None, None] + beta[None, :, None, None]

        def _gconv1x1(t, w):
            b, c, h, ww = t.shape
            o = jnp.einsum('bgci,goc->bgoi', t.reshape(b, GROUPS, c // GROUPS, h * ww), w)
            return o.reshape(b, GROUPS * w.shape[1], h, ww)

        def _grid_sample(img, grid):
            N, Ci, Hi, Wi = img.shape
            gx = (grid[..., 0] + 1.0) * (Wi / 2.0) - 0.5
            gy = (grid[..., 1] + 1.0) * (Hi / 2.0) - 0.5
            x0 = jnp.floor(gx)
            y0 = jnp.floor(gy)
            wx = gx - x0
            wy = gy - y0

            def gather(im, ix, iy):
                valid = (ix >= 0) & (ix < Wi) & (iy >= 0) & (iy < Hi)
                ixc = jnp.clip(ix, 0, Wi - 1).astype(jnp.int32)
                iyc = jnp.clip(iy, 0, Hi - 1).astype(jnp.int32)
                return im[:, iyc, ixc] * valid[None].astype(im.dtype)

            def sample_one(im, x0, y0, wx, wy):
                v00 = gather(im, x0, y0)
                v01 = gather(im, x0 + 1, y0)
                v10 = gather(im, x0, y0 + 1)
                v11 = gather(im, x0 + 1, y0 + 1)
                wx = wx[None]
                wy = wy[None]
                return v00 * (1 - wx) * (1 - wy) + v01 * wx * (1 - wy) + v10 * (1 - wx) * wy + v11 * wx * wy
            return jax.vmap(sample_one)(img, x0, y0, wx, wy)

        def _forward(x, bn1_g, bn1_b, bn2_g, bn2_b, qw, kw, vw, out_w, out_b, off_dw_w, off_dw_b, off_pw_w, cpb_w1, cpb_b1, cpb_w2, cpb_b2, cpb_w3, cpb_b3, mlp_w1, mlp_b1, mlp_w2, mlp_b2):
            b = x.shape[0]
            xn = _bn(x, bn1_g, bn1_b)
            q = _gconv1x1(xn, qw)
            qg = q.reshape(b * GROUPS, DH, H, W)
            off = jax.lax.conv_general_dilated(qg, off_dw_w, (DF, DF), ((1, 1), (1, 1)), dimension_numbers=('NCHW', 'OIHW', 'NCHW'), feature_group_count=DH)
            off = jax.nn.gelu(off + off_dw_b[None, :, None, None], approximate=False)
            off = jnp.tanh(jnp.einsum('bchw,oc->bohw', off, off_pw_w)) * OFF_SCALE
            Hd, Wd = (off.shape[-2], off.shape[-1])
            gy, gx = jnp.meshgrid(jnp.arange(Hd, dtype=x.dtype), jnp.arange(Wd, dtype=x.dtype), indexing='ij')
            vx = gx[None] + off[:, 0]
            vy = gy[None] + off[:, 1]
            nx = 2.0 * vx / max(Hd - 1, 1) - 1.0
            ny = 2.0 * vy / max(Wd - 1, 1) - 1.0
            vgrid_scaled = jnp.stack((nx, ny), axis=-1)
            kv = _grid_sample(xn.reshape(b * GROUPS, DH, H, W), vgrid_scaled)
            kv = kv.reshape(b, GROUPS * DH, Hd, Wd)
            k = _gconv1x1(kv, kw)
            v = _gconv1x1(kv, vw)
            scale = DH ** (-0.5)
            qh = q.reshape(b, HEADS, DH, H * W).transpose(0, 1, 3, 2) * scale
            kh = k.reshape(b, HEADS, DH, Hd * Wd).transpose(0, 1, 3, 2)
            vh = v.reshape(b, HEADS, DH, Hd * Wd).transpose(0, 1, 3, 2)
            qgy, qgx = jnp.meshgrid(jnp.arange(H, dtype=x.dtype), jnp.arange(W, dtype=x.dtype), indexing='ij')
            grid_q = jnp.stack((2.0 * qgx / max(H - 1, 1) - 1.0, 2.0 * qgy / max(W - 1, 1) - 1.0), axis=-1).reshape(1, H * W, 2)
            grid_kv = vgrid_scaled.reshape(b * GROUPS, Hd * Wd, 2)
            pos = grid_q[:, :, None, :] - grid_kv[:, None, :, :]
            bias = jnp.sign(pos) * jnp.log1p(jnp.abs(pos))
            bias = jax.nn.relu(bias @ cpb_w1 + cpb_b1)
            bias = jax.nn.relu(bias @ cpb_w2 + cpb_b2)
            bias = (bias @ cpb_w3 + cpb_b3).reshape(b, GROUPS, H * W, Hd * Wd)
            sim = jnp.einsum('bhid,bhjd->bhij', qh, kh) + bias
            attn = jax.nn.softmax(sim, axis=-1)
            out = jnp.einsum('bhij,bhjd->bhid', attn, vh)
            out = out.transpose(0, 1, 3, 2).reshape(b, HEADS * DH, H, W)
            out = jnp.einsum('bchw,oc->bohw', out, out_w) + out_b[None, :, None, None]
            x = x + out
            xn2 = _bn(x, bn2_g, bn2_b)
            h1 = jax.nn.gelu(jnp.einsum('bchw,oc->bohw', xn2, mlp_w1) + mlp_b1[None, :, None, None], approximate=False)
            return x + jnp.einsum('bchw,oc->bohw', h1, mlp_w2) + mlp_b2[None, :, None, None]
        ks = jax.random.split(jax.random.key(seed), 16)
        w = lambda k, shape: jax.random.normal(k, shape, dtype=jnp.float32) * 0.02
        return {'x': jax.random.normal(ks[0], (B, C, H, W), dtype=jnp.float32), 'bn1_g': jnp.ones((C,), jnp.float32), 'bn1_b': jnp.zeros((C,), jnp.float32), 'bn2_g': jnp.ones((C,), jnp.float32), 'bn2_b': jnp.zeros((C,), jnp.float32), 'qw': w(ks[1], (GROUPS, DH, C // GROUPS)), 'kw': w(ks[2], (GROUPS, DH, C // GROUPS)), 'vw': w(ks[3], (GROUPS, DH, C // GROUPS)), 'out_w': w(ks[4], (C, HEADS * DH)), 'out_b': jnp.zeros((C,), jnp.float32), 'off_dw_w': w(ks[5], (DH, 1, 6, 6)), 'off_dw_b': jnp.zeros((DH,), jnp.float32), 'off_pw_w': w(ks[6], (2, DH)), 'cpb_w1': w(ks[7], (2, 32)), 'cpb_b1': jnp.zeros((32,), jnp.float32), 'cpb_w2': w(ks[8], (32, 32)), 'cpb_b2': jnp.zeros((32,), jnp.float32), 'cpb_w3': w(ks[9], (32, 1)), 'cpb_b3': jnp.zeros((1,), jnp.float32), 'mlp_w1': w(ks[10], (4 * C, C)), 'mlp_b1': jnp.zeros((4 * C,), jnp.float32), 'mlp_w2': w(ks[11], (C, 4 * C)), 'mlp_b2': jnp.zeros((C,), jnp.float32)}
    _L1_conv_all = _L1_conv_setup()
    _L1_conv_in = {k: v for k, v in _L1_conv_all.items() if k in ('bn1_g', 'bn1_b', 'bn2_g', 'bn2_b', 'qw', 'kw', 'vw', 'out_w', 'out_b', 'off_dw_w', 'off_dw_b', 'off_pw_w', 'cpb_w1', 'cpb_b1', 'cpb_w2', 'cpb_b2', 'cpb_w3', 'cpb_b3', 'mlp_w1', 'mlp_b1', 'mlp_w2', 'mlp_b2')}
    del _L1_conv_all
    return {'x': x, 'L0_conv_bn1_g': _L0_conv_in['bn1_g'], 'L0_conv_bn1_b': _L0_conv_in['bn1_b'], 'L0_conv_bn2_g': _L0_conv_in['bn2_g'], 'L0_conv_bn2_b': _L0_conv_in['bn2_b'], 'L0_conv_qw': _L0_conv_in['qw'], 'L0_conv_kw': _L0_conv_in['kw'], 'L0_conv_vw': _L0_conv_in['vw'], 'L0_conv_out_w': _L0_conv_in['out_w'], 'L0_conv_out_b': _L0_conv_in['out_b'], 'L0_conv_off_dw_w': _L0_conv_in['off_dw_w'], 'L0_conv_off_dw_b': _L0_conv_in['off_dw_b'], 'L0_conv_off_pw_w': _L0_conv_in['off_pw_w'], 'L0_conv_cpb_w1': _L0_conv_in['cpb_w1'], 'L0_conv_cpb_b1': _L0_conv_in['cpb_b1'], 'L0_conv_cpb_w2': _L0_conv_in['cpb_w2'], 'L0_conv_cpb_b2': _L0_conv_in['cpb_b2'], 'L0_conv_cpb_w3': _L0_conv_in['cpb_w3'], 'L0_conv_cpb_b3': _L0_conv_in['cpb_b3'], 'L0_conv_mlp_w1': _L0_conv_in['mlp_w1'], 'L0_conv_mlp_b1': _L0_conv_in['mlp_b1'], 'L0_conv_mlp_w2': _L0_conv_in['mlp_w2'], 'L0_conv_mlp_b2': _L0_conv_in['mlp_b2'], 'L1_conv_bn1_g': _L1_conv_in['bn1_g'], 'L1_conv_bn1_b': _L1_conv_in['bn1_b'], 'L1_conv_bn2_g': _L1_conv_in['bn2_g'], 'L1_conv_bn2_b': _L1_conv_in['bn2_b'], 'L1_conv_qw': _L1_conv_in['qw'], 'L1_conv_kw': _L1_conv_in['kw'], 'L1_conv_vw': _L1_conv_in['vw'], 'L1_conv_out_w': _L1_conv_in['out_w'], 'L1_conv_out_b': _L1_conv_in['out_b'], 'L1_conv_off_dw_w': _L1_conv_in['off_dw_w'], 'L1_conv_off_dw_b': _L1_conv_in['off_dw_b'], 'L1_conv_off_pw_w': _L1_conv_in['off_pw_w'], 'L1_conv_cpb_w1': _L1_conv_in['cpb_w1'], 'L1_conv_cpb_b1': _L1_conv_in['cpb_b1'], 'L1_conv_cpb_w2': _L1_conv_in['cpb_w2'], 'L1_conv_cpb_b2': _L1_conv_in['cpb_b2'], 'L1_conv_cpb_w3': _L1_conv_in['cpb_w3'], 'L1_conv_cpb_b3': _L1_conv_in['cpb_b3'], 'L1_conv_mlp_w1': _L1_conv_in['mlp_w1'], 'L1_conv_mlp_b1': _L1_conv_in['mlp_b1'], 'L1_conv_mlp_w2': _L1_conv_in['mlp_w2'], 'L1_conv_mlp_b2': _L1_conv_in['mlp_b2']}

def reference(x, L0_conv_bn1_g, L0_conv_bn1_b, L0_conv_bn2_g, L0_conv_bn2_b, L0_conv_qw, L0_conv_kw, L0_conv_vw, L0_conv_out_w, L0_conv_out_b, L0_conv_off_dw_w, L0_conv_off_dw_b, L0_conv_off_pw_w, L0_conv_cpb_w1, L0_conv_cpb_b1, L0_conv_cpb_w2, L0_conv_cpb_b2, L0_conv_cpb_w3, L0_conv_cpb_b3, L0_conv_mlp_w1, L0_conv_mlp_b1, L0_conv_mlp_w2, L0_conv_mlp_b2, L1_conv_bn1_g, L1_conv_bn1_b, L1_conv_bn2_g, L1_conv_bn2_b, L1_conv_qw, L1_conv_kw, L1_conv_vw, L1_conv_out_w, L1_conv_out_b, L1_conv_off_dw_w, L1_conv_off_dw_b, L1_conv_off_pw_w, L1_conv_cpb_w1, L1_conv_cpb_b1, L1_conv_cpb_w2, L1_conv_cpb_b2, L1_conv_cpb_w3, L1_conv_cpb_b3, L1_conv_mlp_w1, L1_conv_mlp_b1, L1_conv_mlp_w2, L1_conv_mlp_b2):
    import jax
    import jax.numpy as jnp

    def _L0_conv_ref(x, bn1_g, bn1_b, bn2_g, bn2_b, qw, kw, vw, out_w, out_b, off_dw_w, off_dw_b, off_pw_w, cpb_w1, cpb_b1, cpb_w2, cpb_b2, cpb_w3, cpb_b3, mlp_w1, mlp_b1, mlp_w2, mlp_b2):
        import jax, jax.numpy as jnp
        import numpy as np
        B, C, H, W = (2, 128, 32, 32)
        HEADS = 8
        GROUPS = 8
        DH = 16
        DF = 4
        OFF_SCALE = 4.0
        EPS = 1e-05

        def _bn(t, gamma, beta):
            s = gamma / jnp.sqrt(1.0 + EPS)
            return t * s[None, :, None, None] + beta[None, :, None, None]

        def _gconv1x1(t, w):
            b, c, h, ww = t.shape
            o = jnp.einsum('bgci,goc->bgoi', t.reshape(b, GROUPS, c // GROUPS, h * ww), w)
            return o.reshape(b, GROUPS * w.shape[1], h, ww)

        def _grid_sample(img, grid):
            N, Ci, Hi, Wi = img.shape
            gx = (grid[..., 0] + 1.0) * (Wi / 2.0) - 0.5
            gy = (grid[..., 1] + 1.0) * (Hi / 2.0) - 0.5
            x0 = jnp.floor(gx)
            y0 = jnp.floor(gy)
            wx = gx - x0
            wy = gy - y0

            def gather(im, ix, iy):
                valid = (ix >= 0) & (ix < Wi) & (iy >= 0) & (iy < Hi)
                ixc = jnp.clip(ix, 0, Wi - 1).astype(jnp.int32)
                iyc = jnp.clip(iy, 0, Hi - 1).astype(jnp.int32)
                return im[:, iyc, ixc] * valid[None].astype(im.dtype)

            def sample_one(im, x0, y0, wx, wy):
                v00 = gather(im, x0, y0)
                v01 = gather(im, x0 + 1, y0)
                v10 = gather(im, x0, y0 + 1)
                v11 = gather(im, x0 + 1, y0 + 1)
                wx = wx[None]
                wy = wy[None]
                return v00 * (1 - wx) * (1 - wy) + v01 * wx * (1 - wy) + v10 * (1 - wx) * wy + v11 * wx * wy
            return jax.vmap(sample_one)(img, x0, y0, wx, wy)

        def _forward(x, bn1_g, bn1_b, bn2_g, bn2_b, qw, kw, vw, out_w, out_b, off_dw_w, off_dw_b, off_pw_w, cpb_w1, cpb_b1, cpb_w2, cpb_b2, cpb_w3, cpb_b3, mlp_w1, mlp_b1, mlp_w2, mlp_b2):
            b = x.shape[0]
            xn = _bn(x, bn1_g, bn1_b)
            q = _gconv1x1(xn, qw)
            qg = q.reshape(b * GROUPS, DH, H, W)
            off = jax.lax.conv_general_dilated(qg, off_dw_w, (DF, DF), ((1, 1), (1, 1)), dimension_numbers=('NCHW', 'OIHW', 'NCHW'), feature_group_count=DH)
            off = jax.nn.gelu(off + off_dw_b[None, :, None, None], approximate=False)
            off = jnp.tanh(jnp.einsum('bchw,oc->bohw', off, off_pw_w)) * OFF_SCALE
            Hd, Wd = (off.shape[-2], off.shape[-1])
            gy, gx = jnp.meshgrid(jnp.arange(Hd, dtype=x.dtype), jnp.arange(Wd, dtype=x.dtype), indexing='ij')
            vx = gx[None] + off[:, 0]
            vy = gy[None] + off[:, 1]
            nx = 2.0 * vx / max(Hd - 1, 1) - 1.0
            ny = 2.0 * vy / max(Wd - 1, 1) - 1.0
            vgrid_scaled = jnp.stack((nx, ny), axis=-1)
            kv = _grid_sample(xn.reshape(b * GROUPS, DH, H, W), vgrid_scaled)
            kv = kv.reshape(b, GROUPS * DH, Hd, Wd)
            k = _gconv1x1(kv, kw)
            v = _gconv1x1(kv, vw)
            scale = DH ** (-0.5)
            qh = q.reshape(b, HEADS, DH, H * W).transpose(0, 1, 3, 2) * scale
            kh = k.reshape(b, HEADS, DH, Hd * Wd).transpose(0, 1, 3, 2)
            vh = v.reshape(b, HEADS, DH, Hd * Wd).transpose(0, 1, 3, 2)
            qgy, qgx = jnp.meshgrid(jnp.arange(H, dtype=x.dtype), jnp.arange(W, dtype=x.dtype), indexing='ij')
            grid_q = jnp.stack((2.0 * qgx / max(H - 1, 1) - 1.0, 2.0 * qgy / max(W - 1, 1) - 1.0), axis=-1).reshape(1, H * W, 2)
            grid_kv = vgrid_scaled.reshape(b * GROUPS, Hd * Wd, 2)
            pos = grid_q[:, :, None, :] - grid_kv[:, None, :, :]
            bias = jnp.sign(pos) * jnp.log1p(jnp.abs(pos))
            bias = jax.nn.relu(bias @ cpb_w1 + cpb_b1)
            bias = jax.nn.relu(bias @ cpb_w2 + cpb_b2)
            bias = (bias @ cpb_w3 + cpb_b3).reshape(b, GROUPS, H * W, Hd * Wd)
            sim = jnp.einsum('bhid,bhjd->bhij', qh, kh) + bias
            attn = jax.nn.softmax(sim, axis=-1)
            out = jnp.einsum('bhij,bhjd->bhid', attn, vh)
            out = out.transpose(0, 1, 3, 2).reshape(b, HEADS * DH, H, W)
            out = jnp.einsum('bchw,oc->bohw', out, out_w) + out_b[None, :, None, None]
            x = x + out
            xn2 = _bn(x, bn2_g, bn2_b)
            h1 = jax.nn.gelu(jnp.einsum('bchw,oc->bohw', xn2, mlp_w1) + mlp_b1[None, :, None, None], approximate=False)
            return x + jnp.einsum('bchw,oc->bohw', h1, mlp_w2) + mlp_b2[None, :, None, None]
        return _forward(x, bn1_g, bn1_b, bn2_g, bn2_b, qw, kw, vw, out_w, out_b, off_dw_w, off_dw_b, off_pw_w, cpb_w1, cpb_b1, cpb_w2, cpb_b2, cpb_w3, cpb_b3, mlp_w1, mlp_b1, mlp_w2, mlp_b2)

    def _L1_conv_ref(x, bn1_g, bn1_b, bn2_g, bn2_b, qw, kw, vw, out_w, out_b, off_dw_w, off_dw_b, off_pw_w, cpb_w1, cpb_b1, cpb_w2, cpb_b2, cpb_w3, cpb_b3, mlp_w1, mlp_b1, mlp_w2, mlp_b2):
        import jax, jax.numpy as jnp
        import numpy as np
        B, C, H, W = (2, 128, 32, 32)
        HEADS = 8
        GROUPS = 8
        DH = 16
        DF = 4
        OFF_SCALE = 4.0
        EPS = 1e-05

        def _bn(t, gamma, beta):
            s = gamma / jnp.sqrt(1.0 + EPS)
            return t * s[None, :, None, None] + beta[None, :, None, None]

        def _gconv1x1(t, w):
            b, c, h, ww = t.shape
            o = jnp.einsum('bgci,goc->bgoi', t.reshape(b, GROUPS, c // GROUPS, h * ww), w)
            return o.reshape(b, GROUPS * w.shape[1], h, ww)

        def _grid_sample(img, grid):
            N, Ci, Hi, Wi = img.shape
            gx = (grid[..., 0] + 1.0) * (Wi / 2.0) - 0.5
            gy = (grid[..., 1] + 1.0) * (Hi / 2.0) - 0.5
            x0 = jnp.floor(gx)
            y0 = jnp.floor(gy)
            wx = gx - x0
            wy = gy - y0

            def gather(im, ix, iy):
                valid = (ix >= 0) & (ix < Wi) & (iy >= 0) & (iy < Hi)
                ixc = jnp.clip(ix, 0, Wi - 1).astype(jnp.int32)
                iyc = jnp.clip(iy, 0, Hi - 1).astype(jnp.int32)
                return im[:, iyc, ixc] * valid[None].astype(im.dtype)

            def sample_one(im, x0, y0, wx, wy):
                v00 = gather(im, x0, y0)
                v01 = gather(im, x0 + 1, y0)
                v10 = gather(im, x0, y0 + 1)
                v11 = gather(im, x0 + 1, y0 + 1)
                wx = wx[None]
                wy = wy[None]
                return v00 * (1 - wx) * (1 - wy) + v01 * wx * (1 - wy) + v10 * (1 - wx) * wy + v11 * wx * wy
            return jax.vmap(sample_one)(img, x0, y0, wx, wy)

        def _forward(x, bn1_g, bn1_b, bn2_g, bn2_b, qw, kw, vw, out_w, out_b, off_dw_w, off_dw_b, off_pw_w, cpb_w1, cpb_b1, cpb_w2, cpb_b2, cpb_w3, cpb_b3, mlp_w1, mlp_b1, mlp_w2, mlp_b2):
            b = x.shape[0]
            xn = _bn(x, bn1_g, bn1_b)
            q = _gconv1x1(xn, qw)
            qg = q.reshape(b * GROUPS, DH, H, W)
            off = jax.lax.conv_general_dilated(qg, off_dw_w, (DF, DF), ((1, 1), (1, 1)), dimension_numbers=('NCHW', 'OIHW', 'NCHW'), feature_group_count=DH)
            off = jax.nn.gelu(off + off_dw_b[None, :, None, None], approximate=False)
            off = jnp.tanh(jnp.einsum('bchw,oc->bohw', off, off_pw_w)) * OFF_SCALE
            Hd, Wd = (off.shape[-2], off.shape[-1])
            gy, gx = jnp.meshgrid(jnp.arange(Hd, dtype=x.dtype), jnp.arange(Wd, dtype=x.dtype), indexing='ij')
            vx = gx[None] + off[:, 0]
            vy = gy[None] + off[:, 1]
            nx = 2.0 * vx / max(Hd - 1, 1) - 1.0
            ny = 2.0 * vy / max(Wd - 1, 1) - 1.0
            vgrid_scaled = jnp.stack((nx, ny), axis=-1)
            kv = _grid_sample(xn.reshape(b * GROUPS, DH, H, W), vgrid_scaled)
            kv = kv.reshape(b, GROUPS * DH, Hd, Wd)
            k = _gconv1x1(kv, kw)
            v = _gconv1x1(kv, vw)
            scale = DH ** (-0.5)
            qh = q.reshape(b, HEADS, DH, H * W).transpose(0, 1, 3, 2) * scale
            kh = k.reshape(b, HEADS, DH, Hd * Wd).transpose(0, 1, 3, 2)
            vh = v.reshape(b, HEADS, DH, Hd * Wd).transpose(0, 1, 3, 2)
            qgy, qgx = jnp.meshgrid(jnp.arange(H, dtype=x.dtype), jnp.arange(W, dtype=x.dtype), indexing='ij')
            grid_q = jnp.stack((2.0 * qgx / max(H - 1, 1) - 1.0, 2.0 * qgy / max(W - 1, 1) - 1.0), axis=-1).reshape(1, H * W, 2)
            grid_kv = vgrid_scaled.reshape(b * GROUPS, Hd * Wd, 2)
            pos = grid_q[:, :, None, :] - grid_kv[:, None, :, :]
            bias = jnp.sign(pos) * jnp.log1p(jnp.abs(pos))
            bias = jax.nn.relu(bias @ cpb_w1 + cpb_b1)
            bias = jax.nn.relu(bias @ cpb_w2 + cpb_b2)
            bias = (bias @ cpb_w3 + cpb_b3).reshape(b, GROUPS, H * W, Hd * Wd)
            sim = jnp.einsum('bhid,bhjd->bhij', qh, kh) + bias
            attn = jax.nn.softmax(sim, axis=-1)
            out = jnp.einsum('bhij,bhjd->bhid', attn, vh)
            out = out.transpose(0, 1, 3, 2).reshape(b, HEADS * DH, H, W)
            out = jnp.einsum('bchw,oc->bohw', out, out_w) + out_b[None, :, None, None]
            x = x + out
            xn2 = _bn(x, bn2_g, bn2_b)
            h1 = jax.nn.gelu(jnp.einsum('bchw,oc->bohw', xn2, mlp_w1) + mlp_b1[None, :, None, None], approximate=False)
            return x + jnp.einsum('bchw,oc->bohw', h1, mlp_w2) + mlp_b2[None, :, None, None]
        return _forward(x, bn1_g, bn1_b, bn2_g, bn2_b, qw, kw, vw, out_w, out_b, off_dw_w, off_dw_b, off_pw_w, cpb_w1, cpb_b1, cpb_w2, cpb_b2, cpb_w3, cpb_b3, mlp_w1, mlp_b1, mlp_w2, mlp_b2)

    def _gn(v, G=32, eps=1e-05):
        B_, C_, H_, W_ = v.shape
        g = v.reshape(B_, G, C_ // G, H_, W_)
        m = jnp.mean(g, axis=(2, 3, 4), keepdims=True)
        s = jnp.var(g, axis=(2, 3, 4), keepdims=True)
        return ((g - m) / jnp.sqrt(s + eps)).reshape(v.shape)

    def _ln_c(v, eps=1e-06):
        m = jnp.mean(v, axis=1, keepdims=True)
        s = jnp.var(v, axis=1, keepdims=True)
        return (v - m) / jnp.sqrt(s + eps)

    def _ln_t(v, eps=1e-05):
        m = jnp.mean(v, axis=-1, keepdims=True)
        s = jnp.var(v, axis=-1, keepdims=True)
        return (v - m) / jnp.sqrt(s + eps)

    def _to_tokens(v):
        B_, C_, H_, W_ = v.shape
        return v.reshape(B_, C_, H_ * W_).transpose(0, 2, 1)

    def _from_tokens(t, like):
        B_, C_, H_, W_ = like.shape
        return t.transpose(0, 2, 1).reshape(B_, C_, H_, W_)
    x = _L0_conv_ref(x, L0_conv_bn1_g, L0_conv_bn1_b, L0_conv_bn2_g, L0_conv_bn2_b, L0_conv_qw, L0_conv_kw, L0_conv_vw, L0_conv_out_w, L0_conv_out_b, L0_conv_off_dw_w, L0_conv_off_dw_b, L0_conv_off_pw_w, L0_conv_cpb_w1, L0_conv_cpb_b1, L0_conv_cpb_w2, L0_conv_cpb_b2, L0_conv_cpb_w3, L0_conv_cpb_b3, L0_conv_mlp_w1, L0_conv_mlp_b1, L0_conv_mlp_w2, L0_conv_mlp_b2)
    x = _L1_conv_ref(x, L1_conv_bn1_g, L1_conv_bn1_b, L1_conv_bn2_g, L1_conv_bn2_b, L1_conv_qw, L1_conv_kw, L1_conv_vw, L1_conv_out_w, L1_conv_out_b, L1_conv_off_dw_w, L1_conv_off_dw_b, L1_conv_off_pw_w, L1_conv_cpb_w1, L1_conv_cpb_b1, L1_conv_cpb_w2, L1_conv_cpb_b2, L1_conv_cpb_w3, L1_conv_cpb_b3, L1_conv_mlp_w1, L1_conv_mlp_b1, L1_conv_mlp_w2, L1_conv_mlp_b2)
    return x

_drawn_inputs = setup_inputs


def setup_inputs(seed=0):
    import zlib

    import numpy as np

    out = dict(_drawn_inputs(seed))
    spreads = {'L0_conv_bn1_g': (1.0, 0.6),
     'L0_conv_bn1_b': (0.0, 0.8),
     'L0_conv_bn2_g': (1.0, 0.6),
     'L0_conv_bn2_b': (0.0, 0.8),
     'L0_conv_out_b': (0.0, 0.1),
     'L0_conv_off_dw_b': (0.0, 0.8),
     'L0_conv_cpb_b1': (0.0, 0.8),
     'L0_conv_cpb_b2': (0.0, 2.0),
     'L0_conv_mlp_b1': (0.0, 0.356),
     'L0_conv_mlp_b2': (0.0, 0.1),
     'L1_conv_bn1_g': (1.0, 0.6),
     'L1_conv_bn1_b': (0.0, 0.8),
     'L1_conv_bn2_g': (1.0, 0.6),
     'L1_conv_bn2_b': (0.0, 0.8),
     'L1_conv_out_b': (0.0, 0.1),
     'L1_conv_off_dw_b': (0.0, 0.8),
     'L1_conv_cpb_b1': (0.0, 2.0),
     'L1_conv_cpb_b2': (0.0, 2.0),
     'L1_conv_mlp_b1': (0.0, 0.346),
     'L1_conv_mlp_b2': (0.0, 0.1)}
    factors = {'L0_conv_qw': 8.0,
     'L0_conv_kw': 8.0,
     'L0_conv_vw': 8.0,
     'L0_conv_out_w': 8.0,
     'L0_conv_off_dw_w': 8.0,
     'L0_conv_off_pw_w': 8.0,
     'L0_conv_cpb_w1': 8.0,
     'L0_conv_cpb_w2': 8.0,
     'L0_conv_cpb_w3': 8.0,
     'L1_conv_qw': 8.0,
     'L1_conv_kw': 8.0,
     'L1_conv_vw': 8.0,
     'L1_conv_out_w': 8.0,
     'L1_conv_off_dw_w': 8.0,
     'L1_conv_off_pw_w': 8.0,
     'L1_conv_cpb_w1': 64.0,
     'L1_conv_cpb_w2': 64.0,
     'L1_conv_cpb_w3': 64.0}
    for name, (base, spread) in spreads.items():
        noise = np.random.default_rng([zlib.crc32(name.encode()), seed]).standard_normal(out[name].shape)
        drawn = base * np.exp(spread * noise) if base else spread * noise
        out[name] = jnp.asarray(drawn.astype(out[name].dtype))
    for name, factor in factors.items():
        out[name] = (out[name] * factor).astype(out[name].dtype)
    return out
```

```python
from contextlib import ExitStack

import numpy as np

import concourse.bass as bass
from concourse import mybir

F32 = mybir.dt.float32
F32R = mybir.dt.float32r
ALU = mybir.AluOpType
ACT = mybir.ActivationFunctionType
AX_X = mybir.AxisListType.X

LAYERS, B, C, H, W = 2, 2, 128, 32, 32
G, DH = 8, 16
HW = H * W
KS, DF = 6, 4
HD = WD = 8
NKV = HD * WD
HID = 32
FF = 4 * C
OFF_SCALE = 4.0
EPS = 1e-05
PAD = H + 2

SEGS = LAYERS * B
PAIRS = G // 2
STEPS = 8
CT = 4
QUAD = 128 // HID
SEG_STEPS = PAIRS * STEPS
ALL_STEPS = SEGS * SEG_STEPS
HALF = HW // 2
CHUNKS = HW // 128
ADD_ON_POOL = (0, 1, 2)
RELU_ON_ACT = (0, 1)

VEC = ["bn1_g", "bn1_b", "bn2_g", "bn2_b", "out_b", "mlp_b2", "dw_b", "w1x", "w1y", "b1", "b2", "b3"]
COLS, _at = {}, 0
for _name, _n in ([(v, 1) for v in VEC] + [("mlp_b1", 4), ("dw_w", KS * KS), ("pw", 2 * 2 * PAIRS), ("qw", 128)]
                  + [("kw", 128), ("vw", 128), ("out_w", 128), ("w2", 128), ("w3", STEPS * 32), ("mlp_w1", FF), ("mlp_w2", FF)]):
    COLS[_name] = (_at, _at + _n)
    _at += _n
WCOLS = _at
EARLY = COLS["qw"][1]
CONST, _at = {}, 0
for _name, _n in [("ident", 128), ("gridq", W), ("gridkv", 2), ("neg_x", 1), ("neg_y", CHUNKS), ("ones", 32), ("own", 2)]:
    CONST[_name] = (_at, _at + _n)
    _at += _n
CCOLS = _at


def plan():
    at = {e: {} for e in ("pe", "act", "dve", "pool")}

    def put(engine, step, stage, n):
        at[engine].setdefault(step, []).append((stage, n))

    def before(seg, steps):
        (s0, s1, s2, s3, s4, s5, s6, s7, s8, s9, s10, s11, s12, s13) = steps
        put("dve", s0, "norm1", seg)
        put("pe", s1, "q", seg)
        put("act", s1, "q_out", seg)
        put("pe", s2, "image_t", seg)
        put("act", s2, "image_t_out", seg)
        put("pool", s1, "conv_products", seg)
        put("dve", s3, "conv_sum", seg)
        put("act", s3, "conv_gelu", seg)
        put("pe", s4, "offset", seg)
        put("act", s4, "offset_tanh", seg)
        put("dve", s5, "positions", seg)
        put("pe", s6, "spread", seg)
        put("act", s6, "features", seg)
        put("act", s6, "spread_out", seg)
        put("dve", s7, "features_sign", seg)
        put("dve", s7, "hats", seg)
        put("pool", s8, "hat_products", seg)
        put("pe", s9, "sample", seg)
        put("dve", s10, "sample_out", seg)
        put("pe", s11, "keys_values", seg)
        put("act", s12, "keys_values_out", seg)
        put("dve", s13, "hidden_terms", PAIRS * seg)

    before(0, [-1] * 14)
    put("pe", -1, "scores_start", 0)
    for seg in range(1, SEGS):
        z = SEG_STEPS * (seg - 1)
        before(seg, [z + k for k in (17, 18, 20, 20, 21, 22, 23, 24, 24, 26, 27, 28, 28, 28)])
    for unit in range(SEGS * PAIRS):
        w = STEPS * (unit + 1)
        if unit + 1 < SEGS * PAIRS:
            put("pe", w, "scores_start", unit + 1)
        if unit % PAIRS != PAIRS - 1:
            put("dve", w - 4, "hidden_terms", unit + 1)
        put("pe", w + 1, "scores_t", unit)
        put("dve", w + 2, "score_max", unit)
        put("pe", w + 3, "max_spread", unit)
        put("dve", w + 4, "max_off", unit)
        put("act", w + 5, "exp", unit)
        if unit % PAIRS == PAIRS - 1:
            seg = unit // PAIRS
            z = w
            for h in range(2):
                put("pe", z + 6 + h, "attend", 2 * seg + h)
                put("dve", z + 7 + h, "divide", 2 * seg + h)
            put("pe", z + 10, "project", seg)
            put("dve", z + 11, "residual1", seg)
            for c in range(FF // 128):
                put("pe", z + 12 + c, "mlp_up", FF // 128 * seg + c)
                put("act", z + 12 + c, "mlp_gelu", FF // 128 * seg + c)
            put("pe", z + 16, "mlp_down", seg)
            put("dve", z + 17, "residual2", seg)
    for steps in at.values():
        for step, found in steps.items():
            if step >= 0:
                found.sort(key=lambda s: (s[0] in ("norm1", "hidden_terms")) - (s[0] == "mlp_down"))
    return at


PLAN = plan()
MISC_STAGES = ("q", "image_t", "offset", "spread", "sample", "keys_values", "scores_t", "max_spread", "attend",
               "project", "mlp_up", "mlp_down")
MISC = [s for step in sorted(PLAN["pe"]) for s in PLAN["pe"][step] if s[0] in MISC_STAGES]


def misc_turn(stage, n):
    return MISC.index((stage, n))


def runs(engine, alone):
    out, start = [], 0
    for g in range(ALL_STEPS):
        cut_behind = g in PLAN[engine] or g % STEPS == alone or (g + 1) % STEPS == alone or g >= ALL_STEPS - 2 or g == 0
        if cut_behind:
            out.append((start, g + 1))
            start = g + 1
    return out


def build(nc, x_in, consts, weights, x_out, features_dram):
    with ExitStack() as ctx:
        def sb(name, shape, dt=F32):
            return ctx.enter_context(nc.sbuf_tensor(name, shape, dt))

        def ps(name):
            return ctx.enter_context(nc.psum_tensor(name, [128, HW], F32))

        def sem(name):
            return ctx.enter_context(nc.semaphore(name))

        const = sb("const", [128, CCOLS])
        wts = [sb(f"wts{l}", [128, WCOLS]) for l in range(LAYERS)]
        x = [sb(f"x{b}", [128, HW]) for b in range(B)]
        scale = sb("scale", [128, LAYERS, 2])
        xn = sb("xn", [128, HW])
        qpad = [sb(f"qpad{p}", [128, PAD, PAD]) for p in range(2)]
        image_t = sb("image_t", [128, CHUNKS, C])
        conv = sb("conv", [128, NKV])
        conv_act = sb("conv_act", [128, NKV])
        tanh = sb("tanh", [128, 2, PAIRS])
        coord = sb("coord", [128, 4, 2 * PAIRS])
        pos = sb("pos", [128, 2 * PAIRS, W])
        pos_abs = sb("pos_abs", [128, 2 * PAIRS, W])
        pos_log = sb("pos_log", [128, 2 * PAIRS, W])
        pos_sign = sb("pos_sign", [128, 2 * PAIRS, W])
        feat = sb("feat", [128, 2 * PAIRS, W])
        hat_x = sb("hat_x", [128, 512])
        hat_xd = sb("hat_xd", [128, 512])
        hat_y = sb("hat_y", [128, CHUNKS, 512])
        bilinear = hat_y
        conv_prod = hat_y[:].rearrange("p k n -> p (k n)")[:, 0:NKV * KS * KS].rearrange("p (o k) -> p o k", k=KS * KS)
        sampled = sb("sampled", [128, 2, NKV])
        keys_t = [sb(f"keys_t{p}", [128, PAIRS, 128]) for p in range(2)]
        values = [sb(f"values{p}", [128, C]) for p in range(2)]
        hx = [sb(f"hx{p}", [128, CT, STEPS, W]) for p in range(2)]
        hy = [sb(f"hy{p}", [128, CT, STEPS, H]) for p in range(2)]
        h1_sum = [sb(f"h1_sum{c}", [128, H, W]) for c in range(CT)]
        h1_hi = [sb(f"h1_hi{c}", [128, HW], F32R) for c in range(CT)]
        h1_lo = [sb(f"h1_lo{c}", [128, HW], F32R) for c in range(CT)]
        h2 = [sb(f"h2_{c}", [128, HW]) for c in range(CT)]
        w2_hi = [sb(f"w2_hi{l}", [128, 128], F32R) for l in range(LAYERS)]
        w2_lo = [sb(f"w2_lo{l}", [128, 128], F32R) for l in range(LAYERS)]
        w3_now = sb("w3_now", [128, 32])
        scores_sb = [sb(f"scores_sb{p}", [128, HW]) for p in range(2)]
        neg_max = sb("neg_max", [128, CHUNKS, 2])
        probs = sb("probs", [128, PAIRS, HW])
        rden = sb("rden", [128, HALF])
        attended = sb("attended", [128, HW])
        xn2 = sb("xn2", [128, HW])
        mlp_h = sb("mlp_h", [128, FF // 128, HW])

        z = [ps(f"z{p}") for p in range(2)]
        scores = ps("scores")
        misc = ps("misc")

        const_loaded = sem("const_loaded")
        x_loaded = [sem(f"x_loaded{b}") for b in range(B)]
        early_loaded = [sem(f"early_loaded{l}") for l in range(LAYERS)]
        late_loaded = [sem(f"late_loaded{l}") for l in range(LAYERS)]
        setup_done = sem("setup_done")
        borders_zeroed = sem("borders_zeroed")
        xn_ready = sem("xn_ready")
        q_ready = sem("q_ready")
        conv_multiplied = sem("conv_multiplied")
        conv_ready = sem("conv_ready")
        gelu_ready = sem("gelu_ready")
        tanh_ready = sem("tanh_ready")
        pos_ready = sem("pos_ready")
        logs_ready = sem("logs_ready")
        feat_ready = sem("feat_ready")
        feat_stored = sem("feat_stored")
        hats_in = sem("hats_in")
        hats_ready = sem("hats_ready")
        bilinear_ready = sem("bilinear_ready")
        feat_loaded = [sem(f"feat_loaded{p}") for p in range(2)]
        terms_ready = sem("terms_ready")
        misc_filled = sem("misc_filled")
        misc_emptied = sem("misc_emptied")
        sum_ready = [sem(f"sum_ready{c}") for c in range(CT)]
        hi_ready = [sem(f"hi_ready{c}") for c in range(CT)]
        lo_ready = [sem(f"lo_ready{c}") for c in range(CT)]
        z_ready = [sem(f"z_ready{c}") for c in range(CT)]
        h2_ready = [sem(f"h2_ready{c}") for c in range(CT)]
        w3_ready = sem("w3_ready")
        bias_added = sem("bias_added")
        scores_copied = sem("scores_copied")
        exp_ready = sem("exp_ready")
        xn2_ready = sem("xn2_ready")
        x_ready = sem("x_ready")
        out_stored = sem("out_stored")
        dve_order = sem("dve_order")
        act_order = sem("act_order")

        def w(l, name):
            a, b = COLS[name]
            return wts[l][:, a:b]

        def cst(name):
            a, b = CONST[name]
            return const[:, a:b]

        def bank(h):
            return slice(HALF * h, HALF * (h + 1))

        block = ctx.enter_context(nc.Block())

        @block.sync
        def _(sp):
            sp.dma_start(x[0][:], x_in[0]).then_inc(x_loaded[0], 16)
            sp.dma_start(wts[0][:, 0:EARLY], weights[0][:, 0:EARLY]).then_inc(early_loaded[0], 16)
            sp.dma_start(const[:], consts).then_inc(const_loaded, 16)
            sp.dma_start(wts[0][:, EARLY:WCOLS], weights[0][:, EARLY:WCOLS]).then_inc(late_loaded[0], 16)
            sp.dma_start(x[1][:], x_in[1]).then_inc(x_loaded[1], 16)
            sp.dma_start(wts[1][:, 0:EARLY], weights[1][:, 0:EARLY]).then_inc(early_loaded[1], 16)
            sp.dma_start(wts[1][:, EARLY:WCOLS], weights[1][:, EARLY:WCOLS]).then_inc(late_loaded[1], 16)
            for unit in range(SEGS * PAIRS):
                seg, pair, p = unit // PAIRS, unit % PAIRS, unit % 2
                if pair == 0:
                    sp.wait_ge(feat_ready, seg + 1)
                    sp.dma_start(features_dram[seg].rearrange("c u k q -> k (c u) q"), feat[:]).then_inc(feat_stored, 16)
                    sp.wait_ge(feat_stored, 16 * (seg + 1))
                if unit >= 2:
                    for c in range(CT):
                        sp.wait_ge(sum_ready[c], STEPS * (unit - 1))
                for xy, dst in ((0, hx[p]), (1, hy[p])):
                    f = features_dram[seg, xy, pair]
                    for r in range(QUAD):
                        src = bass.AP(tensor=f.tensor, offset=f.offset + STEPS * r * W,
                                      ap=[[0, HID], [4 * STEPS * W, CT], [1, STEPS * W]])
                        sp.dma_start(dst[HID * r:HID * (r + 1)].rearrange("p c t q -> p c (t q)"), src)\
                            .then_inc(feat_loaded[p], 16)
            for b in range(B):
                seg = (LAYERS - 1) * B + b
                sp.wait_ge(x_ready, seg + 1)
                sp.dma_start(x_out[b], x[b][:]).then_inc(out_stored, 16)
            sp.wait_ge(out_stored, 16 * B)

        @block.gpsimd
        def _(pool):
            def add_terms(p, c, t, g):
                if not (isinstance(g, int) and g == 0):
                    pool.wait_ge(lo_ready[c], g)
                pool.tensor_tensor(h1_sum[c][:], hx[p][:, c, t].unsqueeze(1).broadcast_to([128, H, W]),
                                   hy[p][:, c, t].unsqueeze(2).broadcast_to([128, H, W]), ALU.add)\
                    .then_inc(sum_ready[c], 1)

            def pick_w3(l, t, g):
                if not (isinstance(g, int) and g == 0):
                    pool.wait_ge(bias_added, g)
                pool.tensor_copy(w3_now[:], w(l, "w3").rearrange("p (t m) -> p t m", t=STEPS)[:, t])\
                    .then_inc(w3_ready, 1)

            def step(unit_now, t_now, unit_next, t_next, g):
                for c in ADD_ON_POOL[:2]:
                    add_terms(unit_next % 2, c, t_next, g + 1)
                pick_w3(unit_now // PAIRS // B, t_now, g)
                for c in ADD_ON_POOL[2:]:
                    add_terms(unit_next % 2, c, t_next, g + 1)

            def conv_products(seg):
                pool.wait_ge(q_ready, seg + 1)
                l = seg // B
                q = qpad[seg % 2][:]
                if seg >= 1:
                    pool.wait_ge(misc_emptied, misc_turn("sample", seg - 1) + 1)
                taps = w(l, "dw_w").rearrange("p (a k) -> p a k", a=1).broadcast_to([128, WD, KS * KS])\
                    .rearrange("p o (a b) -> p o a b", a=KS)
                for oy in range(HD):
                    window = bass.AP(tensor=q.tensor, offset=q.offset + DF * oy * PAD,
                                     ap=[q.ap[0], [DF, WD], [PAD, KS], [1, KS]])
                    out = conv_prod[:, WD * oy:WD * (oy + 1)].rearrange("p o (a b) -> p o a b", a=KS)
                    pool.tensor_tensor(out, window, taps, ALU.mult).then_inc(conv_multiplied, 1)

            def hat_products(seg):
                pool.wait_ge(hats_ready, seg + 1)
                pool.tensor_tensor(bilinear[:], hat_y[:], hat_x[:].unsqueeze(1).broadcast_to([128, CHUNKS, 512]),
                                   ALU.mult).then_inc(bilinear_ready, 1)

            stages = {"conv_products": conv_products, "hat_products": hat_products}
            for p in range(2):
                pool.memset(qpad[p][:], 0.0).then_inc(borders_zeroed, 1)
            pool.wait_ge(early_loaded[0], 16)
            for name, n in PLAN["pool"][-1]:
                stages[name](n)
            pool.wait_ge(terms_ready, 1)
            pool.wait_ge(late_loaded[0], 16)
            for c in ADD_ON_POOL:
                add_terms(0, c, 0, 0)
            for a, b in runs("pool", STEPS - 1):
                unit = a // STEPS
                if a % (SEG_STEPS * B) == 0 and a > 0:
                    pool.wait_ge(late_loaded[a // (SEG_STEPS * B)], 16)
                if b - a > 1:
                    with pool.Fori(a, b) as g:
                        t = g - STEPS * unit
                        step(unit, t, unit, t + 1, g)
                elif a < ALL_STEPS - 1:
                    nxt = a + 1
                    if nxt % STEPS == 0:
                        pool.wait_ge(terms_ready, nxt // STEPS + 1)
                    step(unit, a % STEPS, nxt // STEPS, nxt % STEPS, a)
                else:
                    pick_w3(unit // PAIRS // B, a % STEPS, a)
                for name, n in PLAN["pool"].get(b - 1, []):
                    stages[name](n)

        @block.scalar
        def _(act):
            def relu1(c, g):
                act.wait_ge(sum_ready[c], g + 1)
                if not (isinstance(g, int) and g == 0):
                    act.wait_ge(z_ready[c], g)
                act.activation(h1_hi[c][:], h1_sum[c][:].rearrange("p y x -> p (y x)"), ACT.Relu)\
                    .then_inc(hi_ready[c], 1)

            def relu2(l, c, g):
                act.wait_ge(z_ready[c], g + 1)
                if not (isinstance(g, int) and g == 0):
                    act.wait_ge(bias_added, g)
                act.activation(h2[c][:], z[c % 2][:], ACT.Relu, bias=w(l, "b2")).then_inc(h2_ready[c], 1)

            def copy_scores(unit):
                l, p = unit // PAIRS // B, unit % 2
                act.wait_ge(bias_added, STEPS * (unit + 1))
                if unit >= 2:
                    act.wait_ge(exp_ready, unit - 1)
                act.activation(scores_sb[p][:], scores[:], ACT.Identity, bias=w(l, "b3")).then_inc(scores_copied, 1)

            def step(l, g, last=False, copy_of=None):
                for c in range(CT):
                    if c in RELU_ON_ACT[:1] and not last:
                        relu1(c, g + 1)
                    relu2(l, c, g)
                    if c in RELU_ON_ACT[1:] and not last:
                        relu1(c, g + 1)
                    if c == 1 and copy_of is not None:
                        copy_scores(copy_of)

            def ordered(ins):
                ordered.n += 1
                ins.then_inc(act_order, 1)
                act.wait_ge(act_order, ordered.n)
            ordered.n = 0

            def emptied(ins):
                ins.then_inc(misc_emptied, 1)

            def q_out(seg):
                if seg < 2:
                    act.wait_ge(borders_zeroed, 2)
                act.wait_ge(misc_filled, misc_turn("q", seg) + 1)
                inner = qpad[seg % 2][:, 1:H + 1, 1:W + 1]
                act.activation(inner, misc[:].rearrange("p (y x) -> p y x", y=H), ACT.Copy).then_inc(q_ready, 1)
                act.wait_ge(q_ready, seg + 1)
                act.sem_inc(misc_emptied, 1)

            def image_t_out(seg):
                act.wait_ge(misc_filled, misc_turn("image_t", seg) + 1)
                emptied(act.activation(image_t[:].rearrange("p k c -> p (k c)"), misc[:], ACT.Copy))

            def conv_gelu(seg):
                act.wait_ge(conv_ready, seg + 1)
                act.activation(conv_act[:], conv[:], ACT.Gelu, bias=w(seg // B, "dw_b")).then_inc(gelu_ready, 1)

            def offset_tanh(seg):
                act.wait_ge(misc_filled, misc_turn("offset", seg) + 1)
                emptied(act.activation(tanh[:].rearrange("p c u -> p (c u)"), misc[:, 0:2 * PAIRS], ACT.Tanh))

            def features(seg):
                act.wait_ge(pos_ready, seg + 1)
                ordered(act.activation(pos_abs[:], pos[:], ACT.Abs))
                act.activation(pos_sign[:], pos[:], ACT.Sign).then_inc(logs_ready, 1)
                act.activation(pos_log[:], pos_abs[:], ACT.Ln, bias=1.0).then_inc(logs_ready, 1)

            def spread_out(seg):
                act.wait_ge(misc_filled, misc_turn("spread", seg) + 1)
                act.activation(hat_xd[:], misc[:, bank(0)], ACT.Abs, bias=cst("neg_x")).then_inc(hats_in, 1)
                for k in range(CHUNKS):
                    act.activation(hat_y[:, k], misc[:, bank(1)], ACT.Abs, bias=cst("neg_y")[:, k:k + 1]).then_inc(hats_in, 1)
                act.wait_ge(hats_in, (1 + CHUNKS) * (seg + 1))
                act.sem_inc(misc_emptied, 1)

            def keys_values_out(seg):
                act.wait_ge(misc_filled, misc_turn("keys_values", seg) + 1)
                for u in range(PAIRS):
                    rows = slice(32 * u, 32 * (u + 1))
                    ordered(act.activation(keys_t[seg % 2][rows, u], misc[rows, 0:128], ACT.Copy, scale=DH ** -0.5))
                emptied(act.activation(values[seg % 2][:], misc[:, HALF:HALF + C], ACT.Copy))

            def exp(unit):
                act.wait_ge(misc_emptied, misc_turn("max_spread", unit) + 1)
                if unit >= PAIRS:
                    act.wait_ge(misc_emptied, misc_turn("attend", 2 * (unit // PAIRS) - 1) + 1)
                act.activation(probs[:, unit % PAIRS], scores_sb[unit % 2][:], ACT.Exp).then_inc(exp_ready, 1)

            def mlp_gelu(n):
                seg, c = n // (FF // 128), n % (FF // 128)
                act.wait_ge(misc_filled, misc_turn("mlp_up", n) + 1)
                if seg >= 1:
                    act.wait_ge(misc_emptied, misc_turn("mlp_down", seg - 1) + 1)
                emptied(act.activation(mlp_h[:, c], misc[:], ACT.Gelu, bias=w(seg // B, "mlp_b1")[:, c:c + 1]))

            stages = {"q_out": q_out, "image_t_out": image_t_out, "conv_gelu": conv_gelu, "offset_tanh": offset_tanh,
                      "features": features, "spread_out": spread_out, "keys_values_out": keys_values_out, "exp": exp,
                      "mlp_gelu": mlp_gelu}
            act.wait_ge(const_loaded, 16)
            act.wait_ge(early_loaded[0], 16)
            act.wait_ge(setup_done, 1)
            for name, n in PLAN["act"][-1]:
                stages[name](n)
            act.wait_ge(late_loaded[0], 16)
            for c in RELU_ON_ACT:
                relu1(c, 0)
            for a, b in runs("act", 0):
                l = a // (SEG_STEPS * B)
                if a == SEG_STEPS - STEPS:
                    act.wait_ge(early_loaded[1], 16)
                if b - a > 1:
                    with act.Fori(a, b) as g:
                        step(l, g)
                else:
                    copy_of = a // STEPS - 1 if a % STEPS == 0 and a > 0 else None
                    step(l, a, last=a == ALL_STEPS - 1, copy_of=copy_of)
                for name, n in PLAN["act"].get(b - 1, []):
                    stages[name](n)
            copy_scores(SEGS * PAIRS - 1)
            for g in range(ALL_STEPS, max(PLAN["act"]) + 1):
                for name, n in PLAN["act"].get(g, []):
                    stages[name](n)

        @block.vector
        def _(dve):
            def ordered(ins):
                ordered.n += 1
                ins.then_inc(dve_order, 1)
                dve.wait_ge(dve_order, ordered.n)
            ordered.n = 0

            def first_layer(p, c, t, g):
                total = h1_sum[c][:].rearrange("p y x -> p (y x)")
                start = isinstance(g, int) and g == 0
                if c not in RELU_ON_ACT:
                    dve.wait_ge(sum_ready[c], g + 1)
                    if not start:
                        dve.wait_ge(z_ready[c], g)
                    dve.tensor_scalar(h1_hi[c][:], total, 0.0, None, ALU.max).then_inc(hi_ready[c], 1)
                dve.wait_ge(hi_ready[c], g + 1)
                dve.scalar_tensor_tensor(out=h1_lo[c][:], in0=total, scalar=0.0, in1=h1_hi[c][:].bitcast(F32),
                                         op0=ALU.max, op1=ALU.subtract).then_inc(lo_ready[c], 1)

            def add_terms(p, c, t, g):
                if not (isinstance(g, int) and g == 0):
                    dve.wait_ge(lo_ready[c], g)
                dve.tensor_tensor(h1_sum[c][:], hx[p][:, c, t].unsqueeze(1).broadcast_to([128, H, W]),
                                  hy[p][:, c, t].unsqueeze(2).broadcast_to([128, H, W]), ALU.add)\
                    .then_inc(sum_ready[c], 1)

            def step(p, t, g):
                for c in range(CT):
                    if c not in ADD_ON_POOL:
                        add_terms(p, c, t, g)
                for c in range(CT):
                    first_layer(p, c, t, g)

            def norm1(seg):
                l, b = seg // B, seg % B
                if seg < B:
                    dve.wait_ge(x_loaded[b], 16)
                else:
                    dve.wait_ge(x_ready, seg - B + 1)
                if seg >= 1:
                    dve.wait_ge(misc_emptied, misc_turn("image_t", seg - 1) + 1)
                dve.tensor_scalar(xn[:], x[b][:], scale[:, l, 0:1], w(l, "bn1_b"), ALU.mult, ALU.add)\
                    .then_inc(xn_ready, 1)

            def conv_sum(seg):
                dve.wait_ge(conv_multiplied, HD * (seg + 1))
                if seg >= 1:
                    dve.wait_ge(gelu_ready, seg)
                dve.tensor_reduce(conv[:], conv_prod, AX_X, ALU.add).then_inc(conv_ready, 1)

            def positions(seg):
                dve.wait_ge(misc_emptied, misc_turn("offset", seg) + 1)
                if seg >= 1:
                    dve.wait_ge(misc_emptied, misc_turn("spread", seg - 1) + 1)
                    dve.wait_ge(logs_ready, 2 * seg)
                for xy in range(2):
                    ordered(dve.tensor_scalar(coord[:, 0, PAIRS * xy:PAIRS * (xy + 1)], tanh[:, xy], OFF_SCALE,
                                              cst("gridkv")[:, xy:xy + 1], ALU.mult, ALU.add))
                ordered(dve.tensor_scalar(coord[:, 1], coord[:, 0], 2.0, 1.0 / (HD - 1), ALU.mult, ALU.mult))
                ordered(dve.tensor_scalar(coord[:, 2], coord[:, 1], -1.0, None, ALU.add))
                ordered(dve.tensor_scalar(coord[:, 1], coord[:, 2], 1.0, W / 2.0, ALU.add, ALU.mult))
                ordered(dve.tensor_scalar(coord[:, 3], coord[:, 1], -0.5, None, ALU.add))
                dve.tensor_tensor(pos[:], cst("gridq").unsqueeze(1).broadcast_to([128, 2 * PAIRS, W]),
                                  coord[:, 2].unsqueeze(2).broadcast_to([128, 2 * PAIRS, W]), ALU.subtract)\
                    .then_inc(pos_ready, 1)

            def features_sign(seg):
                dve.wait_ge(logs_ready, 2 * (seg + 1))
                if seg >= 1:
                    dve.wait_ge(feat_stored, 16 * seg)
                dve.tensor_tensor(feat[:], pos_sign[:], pos_log[:], ALU.mult).then_inc(feat_ready, 1)

            def hats(seg):
                dve.wait_ge(hats_in, (1 + CHUNKS) * (seg + 1))
                dve.tensor_scalar(hat_x[:], hat_xd[:], 1.0, 1.0, ALU.min, ALU.subtract)
                dve.tensor_scalar(hat_y[:], hat_y[:], 1.0, 1.0, ALU.min, ALU.subtract).then_inc(hats_ready, 1)

            def sample_out(seg):
                dve.wait_ge(misc_filled, misc_turn("sample", seg) + 1)
                if seg >= 1:
                    dve.wait_ge(misc_emptied, misc_turn("keys_values", seg - 1) + 1)
                dve.tensor_tensor(sampled[:], misc[:, 0:128].rearrange("p (h k) -> p h k", h=2),
                                  cst("own").unsqueeze(2).broadcast_to([128, 2, NKV]), ALU.mult)\
                    .then_inc(misc_emptied, 1)

            def hidden_terms(unit):
                l, p = unit // PAIRS // B, unit % 2
                dve.wait_ge(feat_loaded[p], 16 * 2 * QUAD * (unit // 2 + 1))
                ordered(dve.tensor_scalar(hx[p][:], hx[p][:], w(l, "w1x"), None, ALU.mult))
                dve.tensor_scalar(hy[p][:], hy[p][:], w(l, "w1y"), w(l, "b1"), ALU.mult, ALU.add).then_inc(terms_ready, 1)

            def score_max(unit):
                dve.wait_ge(misc_filled, misc_turn("scores_t", unit) + 1)
                if unit >= 1:
                    dve.wait_ge(misc_emptied, misc_turn("max_spread", unit - 1) + 1)
                dve.tensor_reduce(neg_max[:].rearrange("p k h -> p (k h)"),
                                  misc[:].rearrange("p (n j) -> p n j", j=NKV), AX_X, ALU.max, negate=True)\
                    .then_inc(misc_emptied, 1)

            def max_off(unit):
                dve.wait_ge(misc_filled, misc_turn("max_spread", unit) + 1)
                s = scores_sb[unit % 2]
                dve.tensor_tensor(s[:], s[:], misc[:], ALU.add).then_inc(misc_emptied, 1)

            def divide(n):
                seg, h = n // 2, n % 2
                dve.wait_ge(misc_filled, misc_turn("attend", n) + 1)
                ordered(dve.reciprocal(rden[:], misc[:, bank(1)]))
                if seg >= 1:
                    dve.wait_ge(misc_emptied, misc_turn("project", seg - 1) + 1)
                dve.tensor_tensor(attended[:, bank(h)], misc[:, bank(0)], rden[:], ALU.mult).then_inc(misc_emptied, 1)

            def residual1(seg):
                l, b = seg // B, seg % B
                dve.wait_ge(misc_filled, misc_turn("project", seg) + 1)
                dve.scalar_tensor_tensor(out=x[b][:], in0=misc[:], scalar=w(l, "out_b"), in1=x[b][:],
                                         op0=ALU.add, op1=ALU.add).then_inc(misc_emptied, 1)
                dve.wait_ge(misc_emptied, misc_turn("project", seg) + 1)
                dve.tensor_scalar(xn2[:], x[b][:], scale[:, l, 1:2], w(l, "bn2_b"), ALU.mult, ALU.add)\
                    .then_inc(xn2_ready, 1)

            def residual2(seg):
                l, b = seg // B, seg % B
                dve.wait_ge(misc_filled, misc_turn("mlp_down", seg) + 1)
                dve.scalar_tensor_tensor(out=x[b][:], in0=misc[:], scalar=w(l, "mlp_b2"), in1=x[b][:],
                                         op0=ALU.add, op1=ALU.add).then_inc(x_ready, 1)
                dve.wait_ge(x_ready, seg + 1)
                dve.sem_inc(misc_emptied, 1)

            def set_up(l):
                dve.wait_ge(early_loaded[l], 16)
                for k, name in ((0, "bn1_g"), (1, "bn2_g")):
                    ordered(dve.tensor_scalar(scale[:, l, k:k + 1], w(l, name), float(1.0 / np.sqrt(1.0 + EPS)), None,
                                              ALU.mult))

            def split_w2(l):
                dve.wait_ge(late_loaded[l], 16)
                ordered(dve.tensor_copy(w2_hi[l][:], w(l, "w2")))
                ordered(dve.tensor_tensor(w2_lo[l][:], w(l, "w2"), w2_hi[l][:].bitcast(F32), ALU.subtract))

            stages = {"norm1": norm1, "conv_sum": conv_sum, "positions": positions, "features_sign": features_sign,
                      "hats": hats, "sample_out": sample_out, "hidden_terms": hidden_terms, "score_max": score_max,
                      "max_off": max_off, "divide": divide, "residual1": residual1, "residual2": residual2}
            ordered(dve.memset(keys_t[0][:], 0.0))
            dve.memset(keys_t[1][:], 0.0).then_inc(setup_done, 1)
            dve.wait_ge(const_loaded, 16)
            set_up(0)
            for name, n in PLAN["dve"][-1]:
                stages[name](n)
            split_w2(0)
            set_up(1)
            split_w2(1)
            dve.sem_inc(setup_done, 1)
            step(0, 0, 0)
            for a, b in runs("dve", STEPS - 1):
                unit = a // STEPS
                if b - a > 1:
                    with dve.Fori(a, b) as g:
                        step(unit % 2, g + 1 - STEPS * unit, g + 1)
                elif a < ALL_STEPS - 1:
                    if (a + 1) % STEPS == 0:
                        dve.wait_ge(terms_ready, (a + 1) // STEPS + 1)
                    step((a + 1) // STEPS % 2, (a + 1) % STEPS, a + 1)
                for name, n in PLAN["dve"].get(b - 1, []):
                    stages[name](n)
            for g in range(ALL_STEPS, max(PLAN["dve"]) + 1):
                for name, n in PLAN["dve"].get(g, []):
                    stages[name](n)

        @block.tensor
        def _(pe):
            def layer2(l, c, g):
                pe.wait_ge(lo_ready[c], g + 1)
                pe.wait_ge(hi_ready[c], g + 1)
                if c >= 2:
                    pe.wait_ge(h2_ready[c - 2], g + 1)
                elif not (isinstance(g, int) and g == 0):
                    pe.wait_ge(h2_ready[c + 2], g)
                for h in range(2):
                    out = z[c % 2][:, bank(h)]
                    pe.matmul(out, w2_hi[l][:], h1_hi[c][:, bank(h)], start=True, stop=False)
                    pe.matmul(out, w2_hi[l][:], h1_lo[c][:, bank(h)], start=False, stop=False)
                    ins = pe.matmul(out, w2_lo[l][:], h1_hi[c][:, bank(h)], start=False, stop=True)
                ins.then_inc(z_ready[c], 1)

            def layer3(g, last):
                pe.wait_ge(w3_ready, g + 1)
                for c in range(CT):
                    pe.wait_ge(h2_ready[c], g + 1)
                for h in range(2):
                    for c in range(CT):
                        ins = pe.matmul(scores[32 * c:32 * (c + 1), bank(h)], w3_now[:], h2[c][:, bank(h)],
                                        start=False, stop=last, skip_group_check=True)
                ins.then_inc(bias_added, 1)

            def step(l, g, unit_starts=False):
                for c in range(CT):
                    layer2(l, c, g)
                    if c == 0 and not (isinstance(g, int) and g == 0):
                        layer3(g - 1, unit_starts)

            def turn(stage, n):
                k = misc_turn(stage, n)
                if k:
                    pe.wait_ge(misc_emptied, k)

            def filled(ins):
                ins.then_inc(misc_filled, 1)

            def q(seg):
                pe.wait_ge(xn_ready, seg + 1)
                turn("q", seg)
                for h in range(2):
                    ins = pe.matmul(misc[:, bank(h)], w(seg // B, "qw"), xn[:, bank(h)], start=True, stop=True)
                filled(ins)

            def image_transpose(seg):
                turn("image_t", seg)
                for k in range(CHUNKS):
                    s = slice(128 * k, 128 * (k + 1))
                    ins = pe.transpose(misc[:, s], xn[:, s], cst("ident"))
                filled(ins)

            def offset(seg):
                pe.wait_ge(gelu_ready, seg + 1)
                turn("offset", seg)
                pw = w(seg // B, "pw").rearrange("p (h n) -> p h n", h=2)
                for h in range(2):
                    ins = pe.matmul(misc[NKV * h:NKV * (h + 1), 0:2 * PAIRS], conv_act[:], pw[:, h], start=True, stop=True)
                filled(ins)

            def spread(seg):
                pe.wait_ge(pos_ready, seg + 1)
                turn("spread", seg)
                for n in range(2 * PAIRS):
                    ins = pe.matmul(misc[:, 128 * n:128 * (n + 1)], coord[:, 3, n:n + 1].broadcast_to([128, 128]),
                                    cst("ident"), start=True, stop=True)
                filled(ins)

            def sample(seg):
                pe.wait_ge(bilinear_ready, seg + 1)
                turn("sample", seg)
                for k in range(CHUNKS):
                    for u in range(PAIRS):
                        ins = pe.matmul(misc[32 * u:32 * (u + 1), 0:128], image_t[:, k, 32 * u:32 * (u + 1)],
                                        bilinear[:, k, 128 * u:128 * (u + 1)], start=k == 0, stop=k == CHUNKS - 1)
                filled(ins)

            def keys_values(seg):
                turn("keys_values", seg)
                s = sampled[:].rearrange("p h k -> p (h k)")
                pe.matmul(misc[:, 0:128], w(seg // B, "kw"), s, start=True, stop=True)
                filled(pe.matmul(misc[:, HALF:HALF + C], s, w(seg // B, "vw"), start=True, stop=True))

            def scores_start(unit):
                seg, u = unit // PAIRS, unit % PAIRS
                if unit:
                    pe.wait_ge(scores_copied, unit)
                pe.wait_ge(misc_emptied, misc_turn("keys_values", seg) + 1)
                for h in range(2):
                    pe.matmul(scores[:, bank(h)], keys_t[seg % 2][:, u], qpad[seg % 2][:, 1 + H // 2 * h:1 + H // 2 * (h + 1), 1:W + 1],
                              start=True, stop=False, skip_group_check=True)

            def scores_transpose(unit):
                pe.wait_ge(scores_copied, unit + 1)
                turn("scores_t", unit)
                for k in range(CHUNKS):
                    s = slice(128 * k, 128 * (k + 1))
                    ins = pe.transpose(misc[:, s], scores_sb[unit % 2][:, s], cst("ident"))
                filled(ins)

            def max_spread(unit):
                turn("max_spread", unit)
                for k in range(CHUNKS):
                    for h in range(2):
                        ins = pe.matmul(misc[NKV * h:NKV * (h + 1), 128 * k:128 * (k + 1)],
                                        neg_max[:, k, h:h + 1].broadcast_to([128, NKV]), cst("ident"), start=True, stop=True)
                filled(ins)

            def attend(n):
                seg, h = n // 2, n % 2
                pe.wait_ge(exp_ready, PAIRS * (seg + 1))
                turn("attend", n)
                for u in range(PAIRS):
                    rows = slice(32 * u, 32 * (u + 1))
                    pe.matmul(misc[rows, bank(0)], values[seg % 2][:, rows], probs[:, u, bank(h)], start=True, stop=True)
                for u in range(PAIRS):
                    rows = slice(32 * u, 32 * (u + 1))
                    ins = pe.matmul(misc[rows, bank(1)], cst("ones"), probs[:, u, bank(h)], start=True, stop=True)
                filled(ins)

            def project(seg):
                turn("project", seg)
                for h in range(2):
                    ins = pe.matmul(misc[:, bank(h)], w(seg // B, "out_w"), attended[:, bank(h)], start=True, stop=True)
                filled(ins)

            def mlp_up(n):
                seg, c = n // (FF // 128), n % (FF // 128)
                pe.wait_ge(xn2_ready, seg + 1)
                turn("mlp_up", n)
                for h in range(2):
                    ins = pe.matmul(misc[:, bank(h)], w(seg // B, "mlp_w1")[:, 128 * c:128 * (c + 1)], xn2[:, bank(h)],
                                    start=True, stop=True)
                filled(ins)

            def mlp_down(seg):
                turn("mlp_down", seg)
                for h in range(2):
                    for c in range(FF // 128):
                        ins = pe.matmul(misc[:, bank(h)], w(seg // B, "mlp_w2")[:, 128 * c:128 * (c + 1)], mlp_h[:, c, bank(h)],
                                        start=c == 0, stop=c == FF // 128 - 1)
                filled(ins)

            stages = {"q": q, "image_t": image_transpose, "offset": offset, "spread": spread, "sample": sample,
                      "keys_values": keys_values, "scores_start": scores_start, "scores_t": scores_transpose,
                      "max_spread": max_spread, "attend": attend, "project": project, "mlp_up": mlp_up, "mlp_down": mlp_down}
            pe.wait_ge(const_loaded, 16)
            pe.wait_ge(early_loaded[0], 16)
            for name, n in PLAN["pe"][-1]:
                if name == "keys_values":
                    pe.wait_ge(late_loaded[0], 16)
                stages[name](n)
            pe.wait_ge(setup_done, 2)
            for a, b in runs("pe", 0):
                l = a // (SEG_STEPS * B)
                if a == SEG_STEPS - STEPS:
                    pe.wait_ge(early_loaded[1], 16)
                    pe.wait_ge(late_loaded[1], 16)
                if b - a > 1:
                    with pe.Fori(a, b) as g:
                        step(l, g)
                else:
                    step(l, a, unit_starts=a % STEPS == 0)
                for name, n in PLAN["pe"].get(b - 1, []):
                    stages[name](n)
            layer3(ALL_STEPS - 1, True)
            for g in range(ALL_STEPS, max(PLAN["pe"]) + 1):
                for name, n in PLAN["pe"].get(g, []):
                    stages[name](n)


def lay_out_weights(get):
    out = np.zeros((128, WCOLS), np.float32)

    def put(name, a):
        lo, hi = COLS[name]
        out[:, lo:hi] = np.reshape(a, (128, hi - lo))

    for name in ("bn1_g", "bn1_b", "bn2_g", "bn2_b", "out_b", "mlp_b2"):
        put(name, get(name))
    put("dw_b", np.tile(get("off_dw_b"), G))
    put("w1x", np.tile(get("cpb_w1")[0], QUAD))
    put("w1y", np.tile(get("cpb_w1")[1], QUAD))
    put("b1", np.tile(get("cpb_b1"), QUAD))
    put("b2", np.tile(get("cpb_b2"), QUAD))
    put("b3", np.tile(get("cpb_b3"), 128))
    put("mlp_b1", get("mlp_b1").reshape(FF // 128, 128).T)
    put("dw_w", np.tile(get("off_dw_w").reshape(DH, KS * KS), (G, 1)))
    pw = np.zeros((G, DH, 2, 2, PAIRS), np.float32)
    for g in range(G):
        pw[g, :, g % 2, :, g // 2] = get("off_pw_w").T
    put("pw", pw)
    for name, key in (("qw", "qw"), ("kw", "kw"), ("vw", "vw")):
        a = np.zeros((G, DH, G, DH), np.float32)
        for g in range(G):
            a[g, :, g, :] = get(key)[g].T
        put(name, a)
    put("out_w", get("out_w").T)
    w2 = np.zeros((QUAD, HID, QUAD, HID), np.float32)
    w3 = np.zeros((QUAD, HID, STEPS, 32), np.float32)
    for r in range(QUAD):
        w2[r, :, r, :] = get("cpb_w2")
        for t in range(STEPS):
            w3[r, :, t, STEPS * r + t] = get("cpb_w3")[:, 0]
    put("w2", w2)
    put("w3", w3)
    put("mlp_w1", get("mlp_w1").T)
    put("mlp_w2", get("mlp_w2").reshape(C, FF // 128, 128).transpose(2, 1, 0))
    return out


def constants():
    out = np.zeros((128, CCOLS), np.float32)
    p = np.arange(128)

    def put(name, a):
        lo, hi = CONST[name]
        out[:, lo:hi] = a

    put("ident", np.eye(128))
    grid = (np.float32(2.0) * np.arange(W, dtype=np.float32) / np.float32(W - 1) - np.float32(1.0)).astype(np.float32)
    put("gridq", np.broadcast_to(grid, (128, W)))
    put("gridkv", np.stack([p % NKV % WD, p % NKV // WD], 1))
    put("neg_x", -(p % W)[:, None])
    put("neg_y", -4 * np.arange(CHUNKS)[None, :] - (p // W)[:, None])
    put("ones", p[:, None] // NKV == np.arange(32)[None, :] // DH)
    put("own", (p // DH % 2)[:, None] == np.arange(2)[None, :])
    return out


def kernel(**inputs):
    import concourse.bacc as bacc
    from concourse.bass_utils import run_bass_kernel_spmd

    nc = bacc.Bacc("TRN2", target_bir_lowering=False, num_devices=1)
    weights = np.zeros((LAYERS, 128, WCOLS), np.float32)
    for l in range(LAYERS):
        weights[l] = lay_out_weights(lambda name: np.asarray(inputs[f"L{l}_conv_{name}"]))
    arrays = {"x_dram": np.ascontiguousarray(np.asarray(inputs["x"]).reshape(B, C, HW)),
              "consts_dram": constants(), "weights_dram": weights}
    args = [nc.dram_tensor(n, a.shape, F32, kind="ExternalInput").ap() for n, a in arrays.items()]
    out = nc.dram_tensor("out_dram", (B, C, HW), F32, kind="ExternalOutput").ap()
    features = nc.dram_tensor("features_dram", (SEGS, 2, PAIRS, 2 * NKV, W), F32, kind="Internal").ap()
    build(nc, *args, out, features)
    r = run_bass_kernel_spmd(nc, [arrays], core_ids=[0])
    return r.results[0]["out_dram"].reshape(B, C, H, W)
```

```python
from contextlib import ExitStack

import numpy as np

import concourse.bass as bass
from concourse import mybir

F32 = mybir.dt.float32
F32R = mybir.dt.float32r
ALU = mybir.AluOpType
ACT = mybir.ActivationFunctionType
AX_X = mybir.AxisListType.X

LAYERS, B, C, H, W = 2, 2, 128, 32, 32
G, DH = 8, 16
HW = H * W
KS, DF = 6, 4
HD = WD = 8
NKV = HD * WD
HID = 32
FF = 4 * C
OFF_SCALE = 4.0
EPS = 1e-05
PAD = H + 2

SEGS = LAYERS * B
PAIRS = G // 2
STEPS = 8
CT = 4
QUAD = 128 // HID
SEG_STEPS = PAIRS * STEPS
ALL_STEPS = SEGS * SEG_STEPS
HALF = HW // 2
CHUNKS = HW // 128
ROWS_ON_POOL = (32, 32, 32, 16)
PARTS = [1 + (n < H) for n in ROWS_ON_POOL]
RELU_ON_ACT = (0, 1)

VEC = ["bn1_g", "bn1_b", "bn2_g", "bn2_b", "out_b", "mlp_b2", "dw_b", "w1x", "w1y", "b1", "b2", "b3"]
COLS, _at = {}, 0
for _name, _n in ([(v, 1) for v in VEC] + [("mlp_b1", 4), ("dw_w", KS * KS), ("pw", 2 * 2 * PAIRS), ("qw", 128)]
                  + [("kw", 128), ("vw", 128), ("out_w", 128), ("w2", 128), ("w3", STEPS * 32), ("mlp_w1", FF), ("mlp_w2", FF)]):
    COLS[_name] = (_at, _at + _n)
    _at += _n
WCOLS = _at
EARLY = COLS["qw"][1]
CONST, _at = {}, 0
for _name, _n in [("ident", 128), ("gridq", W), ("gridkv", 2), ("neg_x", 1), ("neg_y", CHUNKS), ("ones", 32), ("own", 2)]:
    CONST[_name] = (_at, _at + _n)
    _at += _n
CCOLS = _at


def plan():
    at = {e: {} for e in ("pe", "act", "dve", "pool")}

    def put(engine, step, stage, n):
        at[engine].setdefault(step, []).append((stage, n))

    def before(seg, z):
        def put_at(engine, step, stage, n):
            put(engine, -1 if seg == 0 else z + step, stage, n)

        put_at("dve", 19, "norm1", seg)
        put_at("pe", 20, "q", seg)
        put_at("act", 20, "q_out", seg)
        for part in range(2):
            put_at("pool", 21, "conv_products", 2 * seg + part)
        put_at("dve", 21, "conv_products", seg)
        put_at("pe", 21, "image_t", seg)
        put_at("act", 21, "image_t_out", seg)
        put_at("dve", 22, "conv_sum", seg)
        put_at("act", 22, "conv_gelu", seg)
        put_at("pe", 23, "offset", seg)
        put_at("act", 23, "offset_tanh", seg)
        put_at("dve", 24, "positions", seg)
        put_at("pe", 25, "spread", seg)
        put_at("act", 25, "features", seg)
        put_at("act", 25, "spread_out", seg)
        put_at("dve", 26, "features_sign", seg)
        for part in range(2):
            n = 2 * seg + part
            put_at("act", 26 + part, "distances", n)
            put_at("dve", 27 + part, "hats", n)
            put_at("dve", 28 + part, "hat_products", n)
            put_at("pool", 28 + part, "hat_products", n)
        put_at("pe", 30, "sample", seg)
        put_at("dve", 31, "sample_out", seg)
        put_at("pe", 31, "keys_values", seg)
        put_at("act", 31, "keys_values_out", seg)

    def softmax(unit, transpose, widen, spread, exp):
        put("pe", transpose, "scores_t", unit)
        put("dve", transpose + 1, "score_max", unit)
        put("act", widen, "widen_max", unit)
        put("pe", spread, "max_spread", unit)
        put("dve", spread + 1, "max_off", unit)
        put("act", exp, "exp", unit)

    def after(seg, z):
        for h in range(2):
            put("pe", z + 6 + h, "attend", 2 * seg + h)
            put("act", z + 6 + h, "attend_out", 2 * seg + h)
        put("dve", z + 9, "reciprocals", seg)
        put("dve", z + 10, "divide", seg)
        put("pe", z + 11, "project", seg)
        put("act", z + 11, "project_out", seg)
        put("dve", z + 12, "residual1", seg)
        for c in range(FF // 128):
            put("pe", z + 14 + c, "mlp_up", FF // 128 * seg + c)
            put("act", z + 14 + c, "mlp_gelu", FF // 128 * seg + c)
        put("pe", z + 18, "mlp_down", seg)
        put("act", z + 18, "mlp_down_out", seg)
        put("dve", z + 19, "residual2", seg)

    before(0, 0)
    put("dve", -1, "hidden_terms", 0)
    put("pe", -1, "scores_start", 0)
    for seg in range(SEGS):
        z = SEG_STEPS * (seg + 1)
        after(seg, z)
    for unit in range(SEGS * PAIRS):
        z = STEPS * (unit + 1)
        softmax(unit, *[z + k for k in {0: (1, 2, 3, 5), 1: (0, 2, 4, 6), 2: (3, 4, 6, 7), 3: (2, 3, 4, 6)}[(unit + 1) % PAIRS]])
        if unit + 1 < SEGS * PAIRS:
            at["pe"].setdefault(z, []).insert(0, ("scores_start", unit + 1))
            put("dve", z - 4 if (unit + 1) % PAIRS else z - 3, "hidden_terms", unit + 1)
    for seg in range(1, SEGS):
        before(seg, SEG_STEPS * (seg - 1))
    return at


PLAN = plan()
MISC_STAGES = ("q", "image_t", "offset", "spread", "sample", "keys_values", "scores_t", "max_spread", "attend",
               "project", "mlp_up", "mlp_down")
MISC = [s for step in sorted(PLAN["pe"]) for s in PLAN["pe"][step] if s[0] in MISC_STAGES]


def misc_turn(stage, n):
    return MISC.index((stage, n))


def runs(engine, alone):
    out, start = [], 0
    for g in range(ALL_STEPS):
        if g in PLAN[engine] or g % STEPS == alone or (g + 1) % STEPS == alone or g >= ALL_STEPS - 2 or g < 2:
            n = g + 1 - start
            if n >= 4:
                out.append((start, n // 2))
                start += n // 2 * 2
            out += [(k, 0) for k in range(start, g + 1)]
            start = g + 1
    return out


def build(nc, x_in, consts, weights, x_out, features_dram):
    with ExitStack() as ctx:
        def sb(name, shape, dt=F32):
            return ctx.enter_context(nc.sbuf_tensor(name, shape, dt))

        def ps(name):
            return ctx.enter_context(nc.psum_tensor(name, [128, HW], F32))

        def sem(name):
            return ctx.enter_context(nc.semaphore(name))

        const = sb("const", [128, CCOLS])
        wts = [sb(f"wts{l}", [128, WCOLS]) for l in range(LAYERS)]
        x = [sb(f"x{b}", [128, HW]) for b in range(B)]
        scale = sb("scale", [128, LAYERS, 2])
        work = sb("work", [128, HW])
        xn = xn2 = attended = work
        qpad = [sb(f"qpad{p}", [128, PAD, PAD]) for p in range(2)]
        image_t = sb("image_t", [128, CHUNKS, C])
        conv = sb("conv", [128, NKV])
        conv_act = sb("conv_act", [128, NKV])
        tanh = sb("tanh", [128, 2, PAIRS])
        coord = sb("coord", [128, 4, 2 * PAIRS])
        pos = sb("pos", [128, 2 * PAIRS, W])
        pos_log = pos_abs = sb("pos_abs", [128, 2 * PAIRS, W])
        feat = pos_sign = sb("pos_sign", [128, 2 * PAIRS, W])
        hat_x = sb("hat_x", [128, 512])
        big = sb("big", [128, FF // 128 * HW])
        mlp_h = big[:].rearrange("p (c n) -> p c n", n=HW)
        hat_y = big[:].rearrange("p (k n) -> p k n", k=CHUNKS)
        bilinear = hat_y
        att_sum = big[:, 0:HW]
        att_den = big[:, HW:2 * HW]
        exp_sums = sb("exp_sums", [128, 64])
        out_raw = big[:, 3 * HW:4 * HW]
        key_y = work[:, 0:512]
        conv_prod = big[:, 0:NKV * KS * KS].rearrange("p (o k) -> p o k", k=KS * KS)
        sampled = sb("sampled", [128, 2, NKV])
        keys_t = [sb(f"keys_t{p}", [128, PAIRS, 128]) for p in range(2)]
        values = [sb(f"values{p}", [128, C]) for p in range(2)]
        hx = [sb(f"hx{p}", [128, CT, STEPS, W]) for p in range(2)]
        hy = [sb(f"hy{p}", [128, CT, STEPS, H]) for p in range(2)]
        h1_sum = [sb(f"h1_sum{c}", [128, H, W]) for c in range(CT)]
        h1_hi = [[sb(f"h1_hi{p}{c}", [128, HW], F32R) for c in range(CT)] for p in range(2)]
        h1_lo = [[sb(f"h1_lo{p}{c}", [128, HW], F32R) for c in range(CT)] for p in range(2)]
        h2 = [sb(f"h2_{c}", [128, HW]) for c in range(CT)]
        w2_hi = [sb(f"w2_hi{l}", [128, 128], F32R) for l in range(LAYERS)]
        w2_lo = [sb(f"w2_lo{l}", [128, 128], F32R) for l in range(LAYERS)]
        w3_now = [sb(f"w3_now{p}", [128, 32]) for p in range(2)]
        scores_sb = sb("scores_sb", [128, HW])
        neg_max = sb("neg_max", [128, CHUNKS * 2])
        neg_max_wide = sb("neg_max_wide", [128, CHUNKS * 2, NKV], F32R)
        ident_r = sb("ident_r", [128, 128], F32R)
        probs = sb("probs", [128, PAIRS, HW])

        z = [ps(f"z{p}") for p in range(2)]
        scores = ps("scores")
        misc = ps("misc")

        const_loaded = sem("const_loaded")
        x_loaded = [sem(f"x_loaded{b}") for b in range(B)]
        early_loaded = [sem(f"early_loaded{l}") for l in range(LAYERS)]
        late_loaded = [sem(f"late_loaded{l}") for l in range(LAYERS)]
        setup_done = sem("setup_done")
        borders_zeroed = sem("borders_zeroed")
        xn_ready = sem("xn_ready")
        q_ready = sem("q_ready")
        conv_multiplied = [sem(f"conv_multiplied{k}") for k in range(2)]
        conv_ready = sem("conv_ready")
        gelu_ready = sem("gelu_ready")
        tanh_ready = sem("tanh_ready")
        pos_ready = sem("pos_ready")
        logs_ready = sem("logs_ready")
        feat_ready = sem("feat_ready")
        feat_stored = sem("feat_stored")
        hats_in = sem("hats_in")
        hats_ready = sem("hats_ready")
        hat_x_ready = sem("hat_x_ready")
        bilinear_ready = [sem(f"bilinear_ready{k}") for k in range(2)]
        distances_ready = sem("distances_ready")
        sums_packed = sem("sums_packed")
        reciprocal_ready = sem("reciprocal_ready")
        reciprocals_spread = sem("reciprocals_spread")
        attended_ready = sem("attended_ready")
        feat_loaded = [sem(f"feat_loaded{p}") for p in range(2)]
        terms_ready = sem("terms_ready")
        misc_filled = sem("misc_filled")
        misc_emptied = sem("misc_emptied")
        sum_ready = [sem(f"sum_ready{c}") for c in range(CT)]
        hi_ready = [sem(f"hi_ready{c}") for c in range(CT)]
        lo_ready = [sem(f"lo_ready{c}") for c in range(CT)]
        z_ready = [sem(f"z_ready{c}") for c in range(CT)]
        h2_ready = [sem(f"h2_ready{c}") for c in range(CT)]
        w3_ready = sem("w3_ready")
        bias_added = sem("bias_added")
        scores_copied = sem("scores_copied")
        max_widened = sem("max_widened")
        exp_ready = sem("exp_ready")
        xn2_ready = sem("xn2_ready")
        x_ready = sem("x_ready")
        out_stored = sem("out_stored")
        dve_order = sem("dve_order")
        act_order = sem("act_order")

        def w(l, name):
            a, b = COLS[name]
            return wts[l][:, a:b]

        def cst(name):
            a, b = CONST[name]
            return const[:, a:b]

        def bank(h):
            return slice(HALF * h, HALF * (h + 1))

        def conv_product(engine, seg, oy):
            q = qpad[seg % 2][:]
            taps = w(seg // B, "dw_w").rearrange("p (a k) -> p a k", a=1).broadcast_to([128, WD, KS * KS])\
                .rearrange("p o (a b) -> p o a b", a=KS)
            window = bass.AP(tensor=q.tensor, offset=q.offset + DF * oy * PAD,
                             ap=[q.ap[0], [DF, WD], [PAD, KS], [1, KS]])
            out = conv_prod[:, WD * oy:WD * (oy + 1)].rearrange("p o (a b) -> p o a b", a=KS)
            return engine.tensor_tensor(out, window, taps, ALU.mult)

        def big_free_for_conv(engine, seg):
            if seg >= B:
                engine.wait_ge(x_ready, seg - B + 1)
            elif seg:
                engine.wait_ge(misc_emptied, misc_turn("sample", seg - 1) + 1)

        block = ctx.enter_context(nc.Block())

        @block.sync
        def _(sp):
            def pack_sums(seg):
                sp.wait_ge(misc_emptied, misc_turn("attend", 2 * seg + 1) + 1)
                den = big[:].tensor
                pitch = big[:].ap[0][0]
                src = bass.AP(tensor=den, offset=big[:].offset + HW, ap=[[DH * pitch, G], [64, HW // 64], [1, 64]])
                sp.dma_start(exp_sums[:], src).then_inc(sums_packed, 16)
                sp.wait_ge(reciprocal_ready, seg + 1)
                for d in range(DH):
                    dst = bass.AP(tensor=den, offset=big[:].offset + HW + d * pitch,
                                  ap=[[DH * pitch, G], [64, HW // 64], [1, 64]])
                    sp.dma_start(dst, exp_sums[:]).then_inc(reciprocals_spread, 16)

            sp.dma_start(x[0][:], x_in[0]).then_inc(x_loaded[0], 16)
            sp.dma_start(wts[0][:, 0:EARLY], weights[0][:, 0:EARLY]).then_inc(early_loaded[0], 16)
            sp.dma_start(const[:], consts).then_inc(const_loaded, 16)
            sp.dma_start(wts[0][:, EARLY:WCOLS], weights[0][:, EARLY:WCOLS]).then_inc(late_loaded[0], 16)
            sp.dma_start(x[1][:], x_in[1]).then_inc(x_loaded[1], 16)
            sp.dma_start(wts[1][:, 0:EARLY], weights[1][:, 0:EARLY]).then_inc(early_loaded[1], 16)
            sp.dma_start(wts[1][:, EARLY:WCOLS], weights[1][:, EARLY:WCOLS]).then_inc(late_loaded[1], 16)
            for unit in range(SEGS * PAIRS):
                seg, pair, p = unit // PAIRS, unit % PAIRS, unit % 2
                if pair == 0:
                    sp.wait_ge(feat_ready, seg + 1)
                    sp.dma_start(features_dram[seg].rearrange("c u k q -> k (c u) q"), feat[:]).then_inc(feat_stored, 16)
                    sp.wait_ge(feat_stored, 16 * (seg + 1))
                if unit >= 2:
                    for c in range(CT):
                        sp.wait_ge(sum_ready[c], PARTS[c] * STEPS * (unit - 1))
                if pair == 2 and seg:
                    pack_sums(seg - 1)
                for xy, dst in ((0, hx[p]), (1, hy[p])):
                    f = features_dram[seg, xy, pair]
                    for r in range(QUAD):
                        src = bass.AP(tensor=f.tensor, offset=f.offset + STEPS * r * W,
                                      ap=[[0, HID], [4 * STEPS * W, CT], [1, STEPS * W]])
                        sp.dma_start(dst[HID * r:HID * (r + 1)].rearrange("p c t q -> p c (t q)"), src)\
                            .then_inc(feat_loaded[p], 16)
            for b in range(B):
                seg = (LAYERS - 1) * B + b
                if b == B - 1:
                    pack_sums(seg)
                sp.wait_ge(x_ready, seg + 1)
                sp.dma_start(x_out[b], x[b][:]).then_inc(out_stored, 16)
            sp.wait_ge(out_stored, 16 * B)

        @block.gpsimd
        def _(pool):
            def add_terms(p, c, t, g):
                if not (isinstance(g, int) and g == 0):
                    pool.wait_ge(lo_ready[c], g)
                n = ROWS_ON_POOL[c]
                pool.tensor_tensor(h1_sum[c][:, 0:n], hx[p][:, c, t].unsqueeze(1).broadcast_to([128, n, W]),
                                   hy[p][:, c, t, 0:n].unsqueeze(2).broadcast_to([128, n, W]), ALU.add)\
                    .then_inc(sum_ready[c], 1)

            def pick_w3(l, t, g, p):
                if not (isinstance(g, int) and g < 2):
                    pool.wait_ge(bias_added, g - 1)
                pool.tensor_copy(w3_now[p][:], w(l, "w3").rearrange("p (t m) -> p t m", t=STEPS)[:, t])\
                    .then_inc(w3_ready, 1)

            def step(unit_now, t_now, unit_next, t_next, g, p):
                for c in range(CT):
                    add_terms(unit_next % 2, c, t_next, g + 1)
                pick_w3(unit_now // PAIRS // B, t_now, g, p)

            def conv_products(n):
                seg, part = n // 2, n % 2
                pool.wait_ge(q_ready, seg + 1)
                big_free_for_conv(pool, seg)
                for oy in (2 * part, 2 * part + 1):
                    conv_product(pool, seg, oy).then_inc(conv_multiplied[0], 1)

            def hat_products(n):
                pool.wait_ge(hats_ready, n + 1)
                for k in (4 * (n % 2), 4 * (n % 2) + 1):
                    pool.tensor_tensor(bilinear[:, k], hat_y[:, k], hat_x[:], ALU.mult).then_inc(bilinear_ready[0], 1)

            stages = {"conv_products": conv_products, "hat_products": hat_products}
            for p in range(2):
                pool.memset(qpad[p][:], 0.0).then_inc(borders_zeroed, 1)
            pool.wait_ge(early_loaded[0], 16)
            for name, n in PLAN["pool"][-1]:
                stages[name](n)
            pool.wait_ge(terms_ready, 1)
            pool.wait_ge(late_loaded[0], 16)
            for c in range(CT):
                add_terms(0, c, 0, 0)
            for a, pairs in runs("pool", STEPS - 1):
                unit = a // STEPS
                if a % (SEG_STEPS * B) == 0 and a > 0:
                    pool.wait_ge(late_loaded[a // (SEG_STEPS * B)], 16)
                if pairs:
                    with pool.Fori(a, a + 2 * pairs - 1, 2) as g:
                        for k in range(2):
                            t = g + k - STEPS * unit
                            step(unit, t, unit, t + 1, g + k, (a + k) % 2)
                elif a < ALL_STEPS - 1:
                    nxt = a + 1
                    if nxt % STEPS == 0:
                        pool.wait_ge(terms_ready, nxt // STEPS + 1)
                    step(unit, a % STEPS, nxt // STEPS, nxt % STEPS, a, a % 2)
                else:
                    pick_w3(unit // PAIRS // B, a % STEPS, a, a % 2)
                for name, n in PLAN["pool"].get(a + max(0, 2 * pairs - 1), []):
                    stages[name](n)

        @block.scalar
        def _(act):
            def relu1(c, g, p):
                act.wait_ge(sum_ready[c], PARTS[c] * (g + 1))
                if not (isinstance(g, int) and g < 2):
                    act.wait_ge(z_ready[c], g - 1)
                act.activation(h1_hi[p][c][:], h1_sum[c][:].rearrange("p y x -> p (y x)"), ACT.Relu)\
                    .then_inc(hi_ready[c], 1)

            def relu2(l, c, g):
                act.wait_ge(z_ready[c], g + 1)
                if not (isinstance(g, int) and g == 0):
                    act.wait_ge(bias_added, g)
                act.activation(h2[c][:], z[c % 2][:], ACT.Relu, bias=w(l, "b2")).then_inc(h2_ready[c], 1)

            def copy_scores(unit):
                l = unit // PAIRS // B
                act.wait_ge(bias_added, STEPS * (unit + 1))
                if unit:
                    act.wait_ge(exp_ready, unit)
                act.activation(scores_sb[:], scores[:], ACT.Identity, bias=w(l, "b3")).then_inc(scores_copied, 1)

            def step(l, g, p, last=False, copy_of=None):
                if not last:
                    for c in RELU_ON_ACT:
                        relu1(c, g + 1, 1 - p)
                for c in range(CT):
                    relu2(l, c, g)
                    if c == 1 and copy_of is not None:
                        copy_scores(copy_of)

            def ordered(ins):
                ordered.n += 1
                ins.then_inc(act_order, 1)
                act.wait_ge(act_order, ordered.n)
            ordered.n = 0

            def emptied(ins):
                ins.then_inc(misc_emptied, 1)

            def q_out(seg):
                if seg < 2:
                    act.wait_ge(borders_zeroed, 2)
                act.wait_ge(misc_filled, misc_turn("q", seg) + 1)
                inner = qpad[seg % 2][:, 1:H + 1, 1:W + 1]
                act.activation(inner, misc[:].rearrange("p (y x) -> p y x", y=H), ACT.Copy).then_inc(q_ready, 1)
                act.wait_ge(q_ready, seg + 1)
                act.sem_inc(misc_emptied, 1)

            def image_t_out(seg):
                act.wait_ge(misc_filled, misc_turn("image_t", seg) + 1)
                emptied(act.activation(image_t[:].rearrange("p k c -> p (k c)"), misc[:], ACT.Copy))

            def conv_gelu(seg):
                act.wait_ge(conv_ready, seg + 1)
                act.activation(conv_act[:], conv[:], ACT.Gelu, bias=w(seg // B, "dw_b")).then_inc(gelu_ready, 1)

            def offset_tanh(seg):
                act.wait_ge(misc_filled, misc_turn("offset", seg) + 1)
                emptied(act.activation(tanh[:].rearrange("p c u -> p (c u)"), misc[:, 0:2 * PAIRS], ACT.Tanh))

            def features(seg):
                act.wait_ge(pos_ready, seg + 1)
                ordered(act.activation(pos_abs[:], pos[:], ACT.Abs))
                if seg:
                    act.wait_ge(feat_stored, 16 * seg)
                act.activation(pos_sign[:], pos[:], ACT.Sign).then_inc(logs_ready, 1)
                act.activation(pos_log[:], pos_abs[:], ACT.Ln, bias=1.0).then_inc(logs_ready, 1)

            def spread_out(seg):
                act.wait_ge(misc_filled, misc_turn("spread", seg) + 1)
                act.activation(hat_x[:], misc[:, bank(0)], ACT.Abs, bias=cst("neg_x")).then_inc(hats_in, 1)
                act.activation(key_y, misc[:, bank(1)], ACT.Copy).then_inc(hats_in, 1)
                act.wait_ge(hats_in, 2 * (seg + 1))
                act.sem_inc(misc_emptied, 1)

            def distances(n):
                act.wait_ge(hats_in, 2 * (n // 2 + 1))
                act.wait_ge(conv_ready, n // 2 + 1)
                for k in range(4 * (n % 2), 4 * (n % 2) + 4):
                    ins = act.activation(hat_y[:, k], key_y, ACT.Abs, bias=cst("neg_y")[:, k:k + 1])
                    if k % 4 < 3:
                        ordered(ins)
                ins.then_inc(distances_ready, 1)

            def attend_out(n):
                seg, h = n // 2, n % 2
                act.wait_ge(misc_filled, misc_turn("attend", n) + 1)
                before = ("sample", seg + 1) if seg + 1 < SEGS else ("mlp_down", seg - 1)
                act.wait_ge(misc_emptied, misc_turn(*before) + 1)
                emptied(act.activation(big[:, 0:2 * HW].rearrange("p (a n) -> p a n", a=2)[:, :, bank(h)],
                                       misc[:].rearrange("p (a n) -> p a n", a=2), ACT.Copy))

            def project_out(seg):
                act.wait_ge(misc_filled, misc_turn("project", seg) + 1)
                emptied(act.activation(out_raw, misc[:], ACT.Identity, bias=w(seg // B, "out_b")))

            def mlp_down_out(seg):
                act.wait_ge(misc_filled, misc_turn("mlp_down", seg) + 1)
                emptied(act.activation(out_raw, misc[:], ACT.Identity, bias=w(seg // B, "mlp_b2")))

            def keys_values_out(seg):
                act.wait_ge(misc_filled, misc_turn("keys_values", seg) + 1)
                for u in range(PAIRS):
                    rows = slice(32 * u, 32 * (u + 1))
                    ordered(act.activation(keys_t[seg % 2][rows, u], misc[rows, 0:128], ACT.Copy, scale=DH ** -0.5))
                emptied(act.activation(values[seg % 2][:], misc[:, HALF:HALF + C], ACT.Copy))

            def widen_max(unit):
                act.wait_ge(misc_emptied, misc_turn("scores_t", unit) + 1)
                if unit:
                    act.wait_ge(misc_filled, misc_turn("max_spread", unit - 1) + 1)
                act.activation(neg_max_wide[:], neg_max[:].unsqueeze(2).broadcast_to([128, 2 * CHUNKS, NKV]), ACT.Copy)\
                    .then_inc(max_widened, 1)

            def exp(unit):
                act.wait_ge(misc_emptied, misc_turn("max_spread", unit) + 1)
                if unit >= PAIRS:
                    act.wait_ge(misc_emptied, misc_turn("attend", 2 * (unit // PAIRS) - 1) + 1)
                act.activation(probs[:, unit % PAIRS], scores_sb[:], ACT.Exp).then_inc(exp_ready, 1)

            def mlp_gelu(n):
                seg, c = n // (FF // 128), n % (FF // 128)
                act.wait_ge(misc_filled, misc_turn("mlp_up", n) + 1)
                act.wait_ge(xn2_ready, seg + 1)
                emptied(act.activation(mlp_h[:, c], misc[:], ACT.Gelu, bias=w(seg // B, "mlp_b1")[:, c:c + 1]))

            stages = {"q_out": q_out, "image_t_out": image_t_out, "conv_gelu": conv_gelu, "offset_tanh": offset_tanh,
                      "features": features, "spread_out": spread_out, "distances": distances, "attend_out": attend_out,
                      "project_out": project_out, "mlp_down_out": mlp_down_out, "keys_values_out": keys_values_out, "exp": exp, "widen_max": widen_max,
                      "mlp_gelu": mlp_gelu}
            act.wait_ge(const_loaded, 16)
            act.wait_ge(early_loaded[0], 16)
            act.wait_ge(setup_done, 1)
            for name, n in PLAN["act"][-1]:
                stages[name](n)
            act.wait_ge(late_loaded[0], 16)
            for c in RELU_ON_ACT:
                relu1(c, 0, 0)
            for a, pairs in runs("act", 0):
                l = a // (SEG_STEPS * B)
                if a == SEG_STEPS - STEPS:
                    act.wait_ge(early_loaded[1], 16)
                if pairs:
                    with act.Fori(a, a + 2 * pairs - 1, 2) as g:
                        for k in range(2):
                            step(l, g + k, (a + k) % 2)
                else:
                    copy_of = a // STEPS - 1 if a % STEPS == 0 and a > 0 else None
                    step(l, a, a % 2, last=a == ALL_STEPS - 1, copy_of=copy_of)
                for name, n in PLAN["act"].get(a + max(0, 2 * pairs - 1), []):
                    stages[name](n)
            copy_scores(SEGS * PAIRS - 1)
            for g in range(ALL_STEPS, max(PLAN["act"]) + 1):
                for name, n in PLAN["act"].get(g, []):
                    stages[name](n)

        @block.vector
        def _(dve):
            def ordered(ins):
                ordered.n += 1
                ins.then_inc(dve_order, 1)
                dve.wait_ge(dve_order, ordered.n)
            ordered.n = 0

            def add_terms(u, c, t, g):
                if not (isinstance(g, int) and g == 0):
                    dve.wait_ge(lo_ready[c], g)
                a = ROWS_ON_POOL[c]
                dve.tensor_tensor(h1_sum[c][:, a:H], hx[u][:, c, t].unsqueeze(1).broadcast_to([128, H - a, W]),
                                  hy[u][:, c, t, a:H].unsqueeze(2).broadcast_to([128, H - a, W]), ALU.add)\
                    .then_inc(sum_ready[c], 1)

            def first_layer(c, g, p):
                total = h1_sum[c][:].rearrange("p y x -> p (y x)")
                if not (isinstance(g, int) and g < 2):
                    dve.wait_ge(z_ready[c], g - 1)
                if c not in RELU_ON_ACT:
                    dve.wait_ge(sum_ready[c], PARTS[c] * (g + 1))
                    dve.tensor_scalar(h1_hi[p][c][:], total, 0.0, None, ALU.max).then_inc(hi_ready[c], 1)
                dve.wait_ge(hi_ready[c], g + 1)
                dve.scalar_tensor_tensor(out=h1_lo[p][c][:], in0=total, scalar=0.0, in1=h1_hi[p][c][:].bitcast(F32),
                                         op0=ALU.max, op1=ALU.subtract).then_inc(lo_ready[c], 1)

            def step(u, t, g, p):
                for c in range(CT):
                    if ROWS_ON_POOL[c] < H:
                        add_terms(u, c, t, g)
                for c in range(CT):
                    first_layer(c, g, p)

            def norm1(seg):
                l, b = seg // B, seg % B
                if seg < B:
                    dve.wait_ge(x_loaded[b], 16)
                else:
                    dve.wait_ge(x_ready, seg - B + 1)
                if seg >= B:
                    dve.wait_ge(misc_emptied, misc_turn("mlp_down", seg - B) + 1)
                elif seg:
                    dve.wait_ge(distances_ready, 2 * seg)
                dve.tensor_scalar(xn[:], x[b][:], scale[:, l, 0:1], w(l, "bn1_b"), ALU.mult, ALU.add)\
                    .then_inc(xn_ready, 1)

            def conv_products(seg):
                dve.wait_ge(q_ready, seg + 1)
                big_free_for_conv(dve, seg)
                for oy in range(HD // 2, HD):
                    conv_product(dve, seg, oy).then_inc(conv_multiplied[1], 1)

            def conv_sum(seg):
                for k in range(2):
                    dve.wait_ge(conv_multiplied[k], HD // 2 * (seg + 1))
                if seg >= 1:
                    dve.wait_ge(gelu_ready, seg)
                dve.tensor_reduce(conv[:], conv_prod, AX_X, ALU.add).then_inc(conv_ready, 1)

            def positions(seg):
                dve.wait_ge(misc_emptied, misc_turn("offset", seg) + 1)
                if seg >= 1:
                    dve.wait_ge(misc_emptied, misc_turn("spread", seg - 1) + 1)
                    dve.wait_ge(logs_ready, 2 * seg)
                for xy in range(2):
                    ordered(dve.tensor_scalar(coord[:, 0, PAIRS * xy:PAIRS * (xy + 1)], tanh[:, xy], OFF_SCALE,
                                              cst("gridkv")[:, xy:xy + 1], ALU.mult, ALU.add))
                ordered(dve.tensor_scalar(coord[:, 1], coord[:, 0], 2.0, 1.0 / (HD - 1), ALU.mult, ALU.mult))
                ordered(dve.tensor_scalar(coord[:, 2], coord[:, 1], -1.0, None, ALU.add))
                ordered(dve.tensor_scalar(coord[:, 1], coord[:, 2], 1.0, W / 2.0, ALU.add, ALU.mult))
                ordered(dve.tensor_scalar(coord[:, 3], coord[:, 1], -0.5, None, ALU.add))
                dve.tensor_tensor(pos[:], cst("gridq").unsqueeze(1).broadcast_to([128, 2 * PAIRS, W]),
                                  coord[:, 2].unsqueeze(2).broadcast_to([128, 2 * PAIRS, W]), ALU.subtract)\
                    .then_inc(pos_ready, 1)

            def features_sign(seg):
                dve.wait_ge(logs_ready, 2 * (seg + 1))
                dve.tensor_tensor(feat[:], pos_sign[:], pos_log[:], ALU.mult).then_inc(feat_ready, 1)

            def hats(n):
                dve.wait_ge(distances_ready, n + 1)
                if n % 2 == 0:
                    dve.tensor_scalar(hat_x[:], hat_x[:], 1.0, 1.0, ALU.min, ALU.subtract).then_inc(hat_x_ready, 1)
                    dve.wait_ge(hat_x_ready, n // 2 + 1)
                y = hat_y[:, 4 * (n % 2):4 * (n % 2) + 4]
                dve.tensor_scalar(y, y, 1.0, 1.0, ALU.min, ALU.subtract).then_inc(hats_ready, 1)

            def hat_products(n):
                dve.wait_ge(hats_ready, n + 1)
                for k in (4 * (n % 2) + 2, 4 * (n % 2) + 3):
                    dve.tensor_tensor(bilinear[:, k], hat_y[:, k], hat_x[:], ALU.mult).then_inc(bilinear_ready[1], 1)

            def sample_out(seg):
                dve.wait_ge(misc_filled, misc_turn("sample", seg) + 1)
                if seg >= 1:
                    dve.wait_ge(misc_emptied, misc_turn("keys_values", seg - 1) + 1)
                dve.tensor_tensor(sampled[:], misc[:, 0:128].rearrange("p (h k) -> p h k", h=2),
                                  cst("own").unsqueeze(2).broadcast_to([128, 2, NKV]), ALU.mult)\
                    .then_inc(misc_emptied, 1)

            def hidden_terms(unit):
                l, p = unit // PAIRS // B, unit % 2
                dve.wait_ge(feat_loaded[p], 16 * 2 * QUAD * (unit // 2 + 1))
                ordered(dve.tensor_scalar(hx[p][:], hx[p][:], w(l, "w1x"), None, ALU.mult))
                dve.tensor_scalar(hy[p][:], hy[p][:], w(l, "w1y"), w(l, "b1"), ALU.mult, ALU.add).then_inc(terms_ready, 1)

            def score_max(unit):
                dve.wait_ge(misc_filled, misc_turn("scores_t", unit) + 1)
                if unit:
                    dve.wait_ge(max_widened, unit)
                dve.tensor_reduce(neg_max[:],
                                  misc[:].rearrange("p (n j) -> p n j", j=NKV), AX_X, ALU.max, negate=True)\
                    .then_inc(misc_emptied, 1)

            def max_off(unit):
                dve.wait_ge(misc_filled, misc_turn("max_spread", unit) + 1)
                s = scores_sb
                dve.tensor_tensor(s[:], s[:], misc[:], ALU.add).then_inc(misc_emptied, 1)

            def reciprocals(seg):
                dve.wait_ge(sums_packed, 16 * (seg + 1))
                dve.reciprocal(exp_sums[:], exp_sums[:]).then_inc(reciprocal_ready, 1)

            def divide(seg):
                dve.wait_ge(reciprocals_spread, 16 * 16 * (seg + 1))
                if seg + 1 < SEGS:
                    dve.wait_ge(distances_ready, 2 * (seg + 2))
                else:
                    dve.wait_ge(misc_emptied, misc_turn("mlp_down", seg - 1) + 1)
                dve.tensor_tensor(attended[:], att_sum, att_den, ALU.mult).then_inc(attended_ready, 1)

            def residual1(seg):
                l, b = seg // B, seg % B
                dve.wait_ge(misc_emptied, misc_turn("project", seg) + 1)
                ordered(dve.tensor_tensor(x[b][:], x[b][:], out_raw, ALU.add))
                dve.tensor_scalar(xn2[:], x[b][:], scale[:, l, 1:2], w(l, "bn2_b"), ALU.mult, ALU.add)\
                    .then_inc(xn2_ready, 1)

            def residual2(seg):
                b = seg % B
                dve.wait_ge(misc_emptied, misc_turn("mlp_down", seg) + 1)
                dve.tensor_tensor(x[b][:], x[b][:], out_raw, ALU.add).then_inc(x_ready, 1)

            def set_up(l):
                dve.wait_ge(early_loaded[l], 16)
                for k, name in ((0, "bn1_g"), (1, "bn2_g")):
                    ordered(dve.tensor_scalar(scale[:, l, k:k + 1], w(l, name), float(1.0 / np.sqrt(1.0 + EPS)), None,
                                              ALU.mult))

            def split_w2(l):
                dve.wait_ge(late_loaded[l], 16)
                ordered(dve.tensor_copy(w2_hi[l][:], w(l, "w2")))
                ordered(dve.tensor_tensor(w2_lo[l][:], w(l, "w2"), w2_hi[l][:].bitcast(F32), ALU.subtract))

            stages = {"norm1": norm1, "conv_sum": conv_sum, "positions": positions, "features_sign": features_sign,
                      "hats": hats, "conv_products": conv_products, "hat_products": hat_products, "sample_out": sample_out, "hidden_terms": hidden_terms, "score_max": score_max,
                      "max_off": max_off, "divide": divide, "reciprocals": reciprocals, "residual1": residual1, "residual2": residual2}
            ordered(dve.memset(keys_t[0][:], 0.0))
            dve.memset(keys_t[1][:], 0.0).then_inc(setup_done, 1)
            dve.wait_ge(const_loaded, 16)
            ordered(dve.tensor_copy(ident_r[:], cst("ident")))
            set_up(0)
            for name, n in PLAN["dve"][-1]:
                stages[name](n)
            split_w2(0)
            set_up(1)
            split_w2(1)
            dve.sem_inc(setup_done, 1)
            step(0, 0, 0, 0)
            for a, pairs in runs("dve", STEPS - 1):
                unit = a // STEPS
                if pairs:
                    with dve.Fori(a, a + 2 * pairs - 1, 2) as g:
                        for k in range(2):
                            step(unit % 2, g + (k + 1 - STEPS * unit), g + (k + 1), (a + k + 1) % 2)
                elif a < ALL_STEPS - 1:
                    if (a + 1) % STEPS == 0:
                        dve.wait_ge(terms_ready, (a + 1) // STEPS + 1)
                    step((a + 1) // STEPS % 2, (a + 1) % STEPS, a + 1, (a + 1) % 2)
                for name, n in PLAN["dve"].get(a + max(0, 2 * pairs - 1), []):
                    stages[name](n)
            for g in range(ALL_STEPS, max(PLAN["dve"]) + 1):
                for name, n in PLAN["dve"].get(g, []):
                    stages[name](n)

        @block.tensor
        def _(pe):
            def layer2(l, c, g, p):
                pe.wait_ge(lo_ready[c], g + 1)
                pe.wait_ge(hi_ready[c], g + 1)
                if c >= 2:
                    pe.wait_ge(h2_ready[c - 2], g + 1)
                elif not (isinstance(g, int) and g == 0):
                    pe.wait_ge(h2_ready[c + 2], g)
                for h in range(2):
                    out = z[c % 2][:, bank(h)]
                    pe.matmul(out, w2_hi[l][:], h1_hi[p][c][:, bank(h)], start=True, stop=False)
                    pe.matmul(out, w2_hi[l][:], h1_lo[p][c][:, bank(h)], start=False, stop=False)
                    ins = pe.matmul(out, w2_lo[l][:], h1_hi[p][c][:, bank(h)], start=False, stop=True)
                ins.then_inc(z_ready[c], 1)

            def layer3(g, p, last):
                pe.wait_ge(w3_ready, g + 1)
                for c in range(CT):
                    pe.wait_ge(h2_ready[c], g + 1)
                for h in range(2):
                    for c in range(CT):
                        ins = pe.matmul(scores[32 * c:32 * (c + 1), bank(h)], w3_now[p][:], h2[c][:, bank(h)],
                                        start=False, stop=last, skip_group_check=True)
                ins.then_inc(bias_added, 1)

            def step(l, g, p, unit_starts=False):
                for c in range(CT):
                    layer2(l, c, g, p)
                    if c == 0 and not (isinstance(g, int) and g == 0):
                        layer3(g - 1, 1 - p, unit_starts)

            def turn(stage, n):
                k = misc_turn(stage, n)
                if k:
                    pe.wait_ge(misc_emptied, k)

            def filled(ins):
                ins.then_inc(misc_filled, 1)

            def q(seg):
                pe.wait_ge(xn_ready, seg + 1)
                turn("q", seg)
                for h in range(2):
                    ins = pe.matmul(misc[:, bank(h)], w(seg // B, "qw"), xn[:, bank(h)], start=True, stop=True)
                filled(ins)

            def image_transpose(seg):
                turn("image_t", seg)
                for k in range(CHUNKS):
                    s = slice(128 * k, 128 * (k + 1))
                    ins = pe.transpose(misc[:, s], xn[:, s], cst("ident"))
                filled(ins)

            def offset(seg):
                pe.wait_ge(gelu_ready, seg + 1)
                turn("offset", seg)
                pw = w(seg // B, "pw").rearrange("p (h n) -> p h n", h=2)
                for h in range(2):
                    ins = pe.matmul(misc[NKV * h:NKV * (h + 1), 0:2 * PAIRS], conv_act[:], pw[:, h], start=True, stop=True)
                filled(ins)

            def spread(seg):
                pe.wait_ge(pos_ready, seg + 1)
                turn("spread", seg)
                for n in range(2 * PAIRS):
                    ins = pe.matmul(misc[:, 128 * n:128 * (n + 1)], coord[:, 3, n:n + 1].broadcast_to([128, 128]),
                                    cst("ident"), start=True, stop=True)
                filled(ins)

            def sample(seg):
                for k in range(2):
                    pe.wait_ge(bilinear_ready[k], 4 * (seg + 1))
                turn("sample", seg)
                for k in range(CHUNKS):
                    for u in range(PAIRS):
                        ins = pe.matmul(misc[32 * u:32 * (u + 1), 0:128], image_t[:, k, 32 * u:32 * (u + 1)],
                                        bilinear[:, k, 128 * u:128 * (u + 1)], start=k == 0, stop=k == CHUNKS - 1)
                filled(ins)

            def keys_values(seg):
                turn("keys_values", seg)
                s = sampled[:].rearrange("p h k -> p (h k)")
                pe.matmul(misc[:, 0:128], w(seg // B, "kw"), s, start=True, stop=True)
                filled(pe.matmul(misc[:, HALF:HALF + C], s, w(seg // B, "vw"), start=True, stop=True))

            def scores_start(unit):
                seg, u = unit // PAIRS, unit % PAIRS
                if unit:
                    pe.wait_ge(scores_copied, unit)
                pe.wait_ge(misc_emptied, misc_turn("keys_values", seg) + 1)
                for h in range(2):
                    pe.matmul(scores[:, bank(h)], keys_t[seg % 2][:, u], qpad[seg % 2][:, 1 + H // 2 * h:1 + H // 2 * (h + 1), 1:W + 1],
                              start=True, stop=False, skip_group_check=True)

            def scores_transpose(unit):
                pe.wait_ge(scores_copied, unit + 1)
                turn("scores_t", unit)
                for k in range(CHUNKS):
                    s = slice(128 * k, 128 * (k + 1))
                    ins = pe.transpose(misc[:, s], scores_sb[:, s], cst("ident"))
                filled(ins)

            def max_spread(unit):
                turn("max_spread", unit)
                pe.wait_ge(max_widened, unit + 1)
                for k in range(CHUNKS):
                    ins = pe.matmul(misc[:, 128 * k:128 * (k + 1)],
                                    neg_max_wide[:, 2 * k:2 * (k + 1)].rearrange("p n j -> p (n j)"),
                                    ident_r[:], start=True, stop=True)
                filled(ins)

            def attend(n):
                seg, h = n // 2, n % 2
                pe.wait_ge(exp_ready, PAIRS * (seg + 1))
                turn("attend", n)
                for u in range(PAIRS):
                    rows = slice(32 * u, 32 * (u + 1))
                    pe.matmul(misc[rows, bank(0)], values[seg % 2][:, rows], probs[:, u, bank(h)], start=True, stop=True)
                for u in range(PAIRS):
                    rows = slice(32 * u, 32 * (u + 1))
                    ins = pe.matmul(misc[rows, bank(1)], cst("ones"), probs[:, u, bank(h)], start=True, stop=True)
                filled(ins)

            def project(seg):
                pe.wait_ge(attended_ready, seg + 1)
                turn("project", seg)
                for h in range(2):
                    ins = pe.matmul(misc[:, bank(h)], w(seg // B, "out_w"), attended[:, bank(h)], start=True, stop=True)
                filled(ins)

            def mlp_up(n):
                seg, c = n // (FF // 128), n % (FF // 128)
                pe.wait_ge(xn2_ready, seg + 1)
                turn("mlp_up", n)
                for h in range(2):
                    ins = pe.matmul(misc[:, bank(h)], w(seg // B, "mlp_w1")[:, 128 * c:128 * (c + 1)], xn2[:, bank(h)],
                                    start=True, stop=True)
                filled(ins)

            def mlp_down(seg):
                turn("mlp_down", seg)
                for h in range(2):
                    for c in range(FF // 128):
                        ins = pe.matmul(misc[:, bank(h)], w(seg // B, "mlp_w2")[:, 128 * c:128 * (c + 1)], mlp_h[:, c, bank(h)],
                                        start=c == 0, stop=c == FF // 128 - 1)
                filled(ins)

            stages = {"q": q, "image_t": image_transpose, "offset": offset, "spread": spread, "sample": sample,
                      "keys_values": keys_values, "scores_start": scores_start, "scores_t": scores_transpose,
                      "max_spread": max_spread, "attend": attend, "project": project, "mlp_up": mlp_up, "mlp_down": mlp_down}
            pe.wait_ge(const_loaded, 16)
            pe.wait_ge(early_loaded[0], 16)
            for name, n in PLAN["pe"][-1]:
                if name == "keys_values":
                    pe.wait_ge(late_loaded[0], 16)
                stages[name](n)
            pe.wait_ge(setup_done, 2)
            for a, pairs in runs("pe", 0):
                l = a // (SEG_STEPS * B)
                if a == SEG_STEPS - STEPS:
                    pe.wait_ge(early_loaded[1], 16)
                    pe.wait_ge(late_loaded[1], 16)
                if pairs:
                    with pe.Fori(a, a + 2 * pairs - 1, 2) as g:
                        for k in range(2):
                            step(l, g + k, (a + k) % 2)
                else:
                    step(l, a, a % 2, unit_starts=a % STEPS == 0)
                for name, n in PLAN["pe"].get(a + max(0, 2 * pairs - 1), []):
                    stages[name](n)
            layer3(ALL_STEPS - 1, (ALL_STEPS - 1) % 2, True)
            for g in range(ALL_STEPS, max(PLAN["pe"]) + 1):
                for name, n in PLAN["pe"].get(g, []):
                    stages[name](n)


def lay_out_weights(get):
    out = np.zeros((128, WCOLS), np.float32)

    def put(name, a):
        lo, hi = COLS[name]
        out[:, lo:hi] = np.reshape(a, (128, hi - lo))

    for name in ("bn1_g", "bn1_b", "bn2_g", "bn2_b", "out_b", "mlp_b2"):
        put(name, get(name))
    put("dw_b", np.tile(get("off_dw_b"), G))
    put("w1x", np.tile(get("cpb_w1")[0], QUAD))
    put("w1y", np.tile(get("cpb_w1")[1], QUAD))
    put("b1", np.tile(get("cpb_b1"), QUAD))
    put("b2", np.tile(get("cpb_b2"), QUAD))
    put("b3", np.tile(get("cpb_b3"), 128))
    put("mlp_b1", get("mlp_b1").reshape(FF // 128, 128).T)
    put("dw_w", np.tile(get("off_dw_w").reshape(DH, KS * KS), (G, 1)))
    pw = np.zeros((G, DH, 2, 2, PAIRS), np.float32)
    for g in range(G):
        pw[g, :, g % 2, :, g // 2] = get("off_pw_w").T
    put("pw", pw)
    for name, key in (("qw", "qw"), ("kw", "kw"), ("vw", "vw")):
        a = np.zeros((G, DH, G, DH), np.float32)
        for g in range(G):
            a[g, :, g, :] = get(key)[g].T
        put(name, a)
    put("out_w", get("out_w").T)
    w2 = np.zeros((QUAD, HID, QUAD, HID), np.float32)
    w3 = np.zeros((QUAD, HID, STEPS, 32), np.float32)
    for r in range(QUAD):
        w2[r, :, r, :] = get("cpb_w2")
        for t in range(STEPS):
            w3[r, :, t, STEPS * r + t] = get("cpb_w3")[:, 0]
    put("w2", w2)
    put("w3", w3)
    put("mlp_w1", get("mlp_w1").T)
    put("mlp_w2", get("mlp_w2").reshape(C, FF // 128, 128).transpose(2, 1, 0))
    return out


def constants():
    out = np.zeros((128, CCOLS), np.float32)
    p = np.arange(128)

    def put(name, a):
        lo, hi = CONST[name]
        out[:, lo:hi] = a

    put("ident", np.eye(128))
    grid = (np.float32(2.0) * np.arange(W, dtype=np.float32) / np.float32(W - 1) - np.float32(1.0)).astype(np.float32)
    put("gridq", np.broadcast_to(grid, (128, W)))
    put("gridkv", np.stack([p % NKV % WD, p % NKV // WD], 1))
    put("neg_x", -(p % W)[:, None])
    put("neg_y", -4 * np.arange(CHUNKS)[None, :] - (p // W)[:, None])
    put("ones", p[:, None] // NKV == np.arange(32)[None, :] // DH)
    put("own", (p // DH % 2)[:, None] == np.arange(2)[None, :])
    return out


def kernel(**inputs):
    import concourse.bacc as bacc
    from concourse.bass_utils import run_bass_kernel_spmd

    nc = bacc.Bacc("TRN2", target_bir_lowering=False, num_devices=1)
    weights = np.zeros((LAYERS, 128, WCOLS), np.float32)
    for l in range(LAYERS):
        weights[l] = lay_out_weights(lambda name: np.asarray(inputs[f"L{l}_conv_{name}"]))
    arrays = {"x_dram": np.ascontiguousarray(np.asarray(inputs["x"]).reshape(B, C, HW)),
              "consts_dram": constants(), "weights_dram": weights}
    args = [nc.dram_tensor(n, a.shape, F32, kind="ExternalInput").ap() for n, a in arrays.items()]
    out = nc.dram_tensor("out_dram", (B, C, HW), F32, kind="ExternalOutput").ap()
    features = nc.dram_tensor("features_dram", (SEGS, 2, PAIRS, 2 * NKV, W), F32, kind="Internal").ap()
    build(nc, *args, out, features)
    r = run_bass_kernel_spmd(nc, [arrays], core_ids=[0])
    return r.results[0]["out_dram"].reshape(B, C, H, W)
```

```python
from contextlib import ExitStack

import numpy as np

import concourse.bass as bass
from concourse import mybir

F32 = mybir.dt.float32
F32R = mybir.dt.float32r
ALU = mybir.AluOpType
ACT = mybir.ActivationFunctionType
AX_X = mybir.AxisListType.X

LAYERS, B, C, H, W = 2, 2, 128, 32, 32
G, DH = 8, 16
HW = H * W
KS, DF = 6, 4
HD = WD = 8
NKV = HD * WD
HID = 32
FF = 4 * C
OFF_SCALE = 4.0
EPS = 1e-05
PAD = H + 2

SEGS = LAYERS * B
PAIRS = G // 2
STEPS = 8
CT = 4
QUAD = 128 // HID
SEG_STEPS = PAIRS * STEPS
ALL_STEPS = SEGS * SEG_STEPS
HALF = HW // 2
CHUNKS = HW // 128
MLP_PARTS = FF // 128
ROWS_ON_POOL = (32, 32, 32, 16)
PARTS = [1 + (n < H) for n in ROWS_ON_POOL]
Z_PARTS = (1, 1, 2, 2)
RELU_ON_ACT = (0, 1)

VEC = ["bn1_g", "bn1_b", "bn2_g", "bn2_b", "out_b", "mlp_b2", "dw_b", "w1x", "w1y", "b1", "b2", "b3"]
COLS, _at = {}, 0
for _name, _n in ([(v, 1) for v in VEC] + [("mlp_b1", 4), ("dw_w", KS * KS), ("pw", 2 * 2 * PAIRS), ("qw", 128)]
                  + [("kw", 128), ("vw", 128), ("out_w", 128), ("w2", 128), ("w3", STEPS * 32), ("mlp_w1", FF), ("mlp_w2", FF)]):
    COLS[_name] = (_at, _at + _n)
    _at += _n
WCOLS = _at
MLP_AT = COLS["mlp_w1"][0]
EARLY = COLS["qw"][1]
CONST, _at = {}, 0
for _name, _n in [("ident", 128), ("gridq", W), ("gridkv", 2), ("neg_x", 1), ("neg_y", CHUNKS), ("ones", 32), ("own", 2)]:
    CONST[_name] = (_at, _at + _n)
    _at += _n
CCOLS = _at


BEFORE_SLOTS = {
    ("dve", "norm1", 0): 19, ("pe", "q", 0): 20, ("act", "q_out", 0): 20, ("pool", "conv_products", 0): 21,
    ("pool", "conv_products", 1): 21, ("dve", "conv_products", 0): 20, ("dve", "conv_products", 1): 21,
    ("pe", "image_t", 0): 21, ("act", "image_t_out", 0): 21, ("dve", "conv_sum", 0): 21,
    ("dve", "conv_sum", 1): 21, ("act", "conv_gelu", 0): 21, ("pe", "offset", 0): 23,
    ("act", "offset_tanh", 0): 23, ("dve", "positions", 0): 24, ("pe", "spread", 0): 25,
    ("act", "features", 0): 25, ("act", "spread_out", 0): 25, ("dve", "features_sign", 0): 25,
    ("act", "distances", 0): 26, ("act", "distances", 1): 26, ("act", "distances", 2): 27,
    ("act", "distances", 3): 28, ("dve", "hats", 0): 27, ("dve", "hats", 1): 29,
    ("pool", "hat_products", 0): 28, ("pool", "hat_products", 1): 30, ("dve", "hat_products", 0): 29,
    ("dve", "hat_products", 1): 29, ("pe", "sample", 0): 30, ("dve", "sample_out", 0): 30,
    ("pe", "keys_values", 0): 31, ("act", "keys_values_out", 0): 31,
}
AFTER_SLOTS = {
    ("pe", "exp_sums", 0): 6, ("act", "exp_sums_out", 0): 6, ("pe", "attend", 0): 7,
    ("act", "attend_out", 0): 7, ("dve", "reciprocal", 0): 8, ("dve", "divide", 0): 9, ("pe", "project", 0): 10,
    ("dve", "residual1", 0): 12, ("pe", "mlp_up", 0): 15, ("act", "mlp_gelu", 0): 15, ("pe", "mlp_up", 1): 16,
    ("act", "mlp_gelu", 1): 16, ("pe", "mlp_up", 2): 17, ("act", "mlp_gelu", 2): 17, ("pe", "mlp_up", 3): 18,
    ("act", "mlp_gelu", 3): 18, ("pe", "mlp_down", 0): 19, ("pe", "mlp_down", 1): 19,
    ("dve", "residual2", 0): 19, ("dve", "residual2", 1): 19,
}
SOFTMAX_STAGES = (("pe", "scores_t"), ("dve", "score_max"), ("act", "widen_max"), ("pe", "max_spread"), ("dve", "max_off"),
                  ("act", "exp"))
SOFTMAX_SLOTS = ((1, 1, 2, 5, 5, 6), (2, 2, 3, 5, 5, 5), (1, 1, 3, 4, 5, 6), (1, 2, 2, 3, 3, 5))
TERMS_SLOTS = ((-6, -3, -5, -6), (-4, -5, -4, -5))
TAIL_SEG = SEGS - 2
LAST = SEGS * PAIRS - 1
TAIL = {
    "pe": [("tail_up", 0), ("scores_t", LAST), ("tail_up", 1), ("tail_up", 2), ("max_spread", LAST), ("tail_up", 3),
           ("exp_sums", SEGS - 1), ("attend", SEGS - 1)] + [("tail_down", c) for c in range(MLP_PARTS)]
          + [("project", SEGS - 1)] + [("tail_up", MLP_PARTS + c) for c in range(MLP_PARTS)]
          + [("tail_down", MLP_PARTS + c) for c in range(MLP_PARTS)],
    "act": [("tail_gelu", 0), ("widen_max", LAST), ("tail_gelu", 1), ("tail_gelu", 2), ("exp", LAST),
            ("exp_sums_out", SEGS - 1), ("attend_out", SEGS - 1)] + [("tail_gelu", n) for n in range(3, 2 * MLP_PARTS)],
    "dve": [("score_max", LAST), ("max_off", LAST), ("reciprocal", SEGS - 1), ("divide", SEGS - 1),
            ("tail_residual2", 0), ("residual1", SEGS - 1), ("tail_residual2", 1), ("tail_residual2", 2)],
}


def plan():
    at = {e: {} for e in ("pe", "act", "dve", "pool")}
    parts = {}
    for (engine, stage, part) in list(BEFORE_SLOTS) + list(AFTER_SLOTS):
        parts[engine, stage] = max(parts.get((engine, stage), 0), part + 1)

    def put(engine, step, stage, n):
        at[engine].setdefault(step, []).append((stage, n))

    late = {"sample_out": -0.5, "keys_values": 0, "keys_values_out": 0}
    for engine, stage, part in BEFORE_SLOTS:
        put(engine, late.get(stage, -1), stage, part)
        if (engine, stage, part) == ("dve", "hats", 0):
            for xy in range(2):
                put("dve", -1, "hidden_terms", xy)
    for seg in range(SEGS - 1):
        for (engine, stage, part), step in AFTER_SLOTS.items():
            if seg < TAIL_SEG or stage not in ("mlp_up", "mlp_gelu", "mlp_down", "residual2"):
                put(engine, SEG_STEPS * (seg + 1) + step, stage, parts[engine, stage] * seg + part)
    for unit in range(SEGS * PAIRS - 1):
        for (engine, stage), step in zip(SOFTMAX_STAGES, SOFTMAX_SLOTS[unit % PAIRS]):
            put(engine, STEPS * (unit + 1) + step, stage, unit)
    for unit in range(1, SEGS * PAIRS):
        for xy in range(2):
            put("dve", STEPS * unit + TERMS_SLOTS[xy][unit % PAIRS], "hidden_terms", 2 * unit + xy)
    for seg in range(1, SEGS):
        for (engine, stage, part), step in BEFORE_SLOTS.items():
            put(engine, SEG_STEPS * (seg - 1) + step, stage, parts[engine, stage] * seg + part)
    for engine, stages in TAIL.items():
        for stage, n in stages:
            put(engine, ALL_STEPS, stage, n)
    return at


PLAN = plan()
MISC_STAGES = ("q", "image_t", "offset", "spread", "sample", "keys_values", "scores_t", "max_spread", "attend", "exp_sums",
               "project", "mlp_up", "mlp_down")
MISC = [s for step in sorted(PLAN["pe"]) for s in PLAN["pe"][step] if s[0] in MISC_STAGES]


def misc_turn(stage, n):
    return MISC.index((stage, n))


def runs(engine, alone):
    out, start = [], 0
    for g in range(ALL_STEPS):
        if g in PLAN[engine] or g % STEPS == alone or (g + 1) % STEPS == alone or g >= ALL_STEPS - 2 or g < 2:
            n = g + 1 - start
            if n >= 4:
                out.append((start, n // 2))
                start += n // 2 * 2
            out += [(k, 0) for k in range(start, g + 1)]
            start = g + 1
    return out


def build(nc, x_in, consts, weights, x_out, features_dram, reciprocals_dram):
    with ExitStack() as ctx:
        def sb(name, shape, dt=F32):
            return ctx.enter_context(nc.sbuf_tensor(name, shape, dt))

        def ps(name):
            return ctx.enter_context(nc.psum_tensor(name, [128, HW], F32))

        def sem(name):
            return ctx.enter_context(nc.semaphore(name))

        const = sb("const", [128, CCOLS])
        wts = [sb(f"wts{l}", [128, MLP_AT]) for l in range(LAYERS)]
        mlp_wts = sb("mlp_wts", [128, WCOLS - MLP_AT])
        x = [sb(f"x{b}", [128, HW]) for b in range(B)]
        scale = sb("scale", [128, LAYERS, 2])
        work = sb("work", [128, HW])
        xn = xn2 = attended = work
        qpad = [sb(f"qpad{p}", [128, PAD, PAD]) for p in range(2)]
        image_t = sb("image_t", [128, CHUNKS, C])
        conv = sb("conv", [128, NKV])
        conv_act = sb("conv_act", [128, NKV])
        tanh = sb("tanh", [128, 2, PAIRS])
        coord = sb("coord", [128, 4, 2 * PAIRS])
        pos = sb("pos", [128, 2 * PAIRS, W])
        pos_log = pos_abs = sb("pos_abs", [128, 2 * PAIRS, W])
        feat = pos_sign = sb("pos_sign", [128, 2 * PAIRS, W])
        hat_x = sb("hat_x", [128, 512])
        big = sb("big", [128, MLP_PARTS * HW])
        mlp_h = big[:].rearrange("p (c n) -> p c n", n=HW)
        hat_y = big[:].rearrange("p (k n) -> p k n", k=CHUNKS)
        bilinear = hat_y
        att_sum = big[:, 0:HW]
        att_den = big[:, HW:2 * HW]
        packed_sums = sb("packed_sums", [128, G * HW // 128])
        key_y = work[:, 0:512]
        conv_prod = big[:, 0:NKV * KS * KS].rearrange("p (o k) -> p o k", k=KS * KS)
        sampled = sb("sampled", [128, 2, NKV])
        keys_t = [sb(f"keys_t{p}", [128, PAIRS, 128]) for p in range(2)]
        values = [sb(f"values{p}", [128, C]) for p in range(2)]
        hx = [sb(f"hx{p}", [128, CT, STEPS, W]) for p in range(2)]
        hy = [sb(f"hy{p}", [128, CT, STEPS, H]) for p in range(2)]
        h1_sum = [sb(f"h1_sum{c}", [128, H, W]) for c in range(CT)]
        h1_hi = [[sb(f"h1_hi{p}{c}", [128, HW], F32R) for c in range(CT)] for p in range(2)]
        h1_lo = [[sb(f"h1_lo{p}{c}", [128, HW], F32R) for c in range(CT)] for p in range(2)]
        h2 = [[sb(f"h2_{c}{p}", [128, HW]) for p in range(2 if c < 2 else 1)] for c in range(CT)]
        w2_hi = [sb(f"w2_hi{l}", [128, 128], F32R) for l in range(LAYERS)]
        w2_lo = [sb(f"w2_lo{l}", [128, 128], F32R) for l in range(LAYERS)]
        w3_now = [sb(f"w3_now{p}", [128, 32]) for p in range(2)]
        neg_max = sb("neg_max", [128, CHUNKS * 2])
        neg_max_wide = sb("neg_max_wide", [128, CHUNKS * 2, NKV], F32R)
        ident_r = sb("ident_r", [128, 128], F32R)
        probs = sb("probs", [128, PAIRS, HW])

        z = [ps(f"z{p}") for p in range(2)]
        scores = ps("scores")
        misc = ps("misc")
        tail_up_to = (z[0], z[1], z[0], z[1], z[0], z[1], scores, misc)
        tail_down_to = (scores, z[0])
        tail_h = [h1_sum[c][:].rearrange("p y x -> p (y x)") for c in range(CT)] + [mlp_h[:, c] for c in range(MLP_PARTS)]

        const_loaded = sem("const_loaded")
        x_loaded = [sem(f"x_loaded{b}") for b in range(B)]
        early_loaded = [sem(f"early_loaded{l}") for l in range(LAYERS)]
        late_loaded = [sem(f"late_loaded{l}") for l in range(LAYERS)]
        mlp_loaded = sem("mlp_loaded")
        setup_done = sem("setup_done")
        borders_zeroed = sem("borders_zeroed")
        xn_ready = sem("xn_ready")
        q_ready = sem("q_ready")
        conv_multiplied = [sem(f"conv_multiplied{k}") for k in range(2)]
        conv_ready = sem("conv_ready")
        gelu_ready = sem("gelu_ready")
        pos_ready = sem("pos_ready")
        logs_ready = sem("logs_ready")
        feat_ready = sem("feat_ready")
        feat_stored = sem("feat_stored")
        hats_in = sem("hats_in")
        hats_ready = sem("hats_ready")
        hat_x_ready = sem("hat_x_ready")
        bilinear_ready = [sem(f"bilinear_ready{k}") for k in range(2)]
        distances_ready = sem("distances_ready")
        feat_loaded = [sem(f"feat_loaded{p}") for p in range(2)]
        terms_ready = sem("terms_ready")
        misc_filled = sem("misc_filled")
        misc_emptied = sem("misc_emptied")
        sum_ready = [sem(f"sum_ready{c}") for c in range(CT)]
        hi_ready = [sem(f"hi_ready{c}") for c in range(CT)]
        lo_ready = [sem(f"lo_ready{c}") for c in range(CT)]
        z_ready = [sem(f"z_ready{c}") for c in range(CT)]
        h2_ready = [sem(f"h2_ready{c}") for c in range(CT)]
        w3_ready = sem("w3_ready")
        bias_added = sem("bias_added")
        scores_copied = sem("scores_copied")
        max_widened = sem("max_widened")
        exp_ready = sem("exp_ready")
        sums_packed = sem("sums_packed")
        reciprocal_ready = sem("reciprocal_ready")
        reciprocals_stored = sem("reciprocals_stored")
        reciprocals_spread = sem("reciprocals_spread")
        attended_ready = sem("attended_ready")
        xn2_ready = sem("xn2_ready")
        x_ready = sem("x_ready")
        tail_up_filled = sem("tail_up_filled")
        tail_gelu_done = sem("tail_gelu_done")
        tail_down_filled = sem("tail_down_filled")
        out_stored = sem("out_stored")
        dve_order = sem("dve_order")
        act_order = sem("act_order")

        def w(l, name):
            a, b = COLS[name]
            return wts[l][:, a:b] if b <= MLP_AT else mlp_wts[:, a - MLP_AT:b - MLP_AT]

        def cst(name):
            a, b = CONST[name]
            return const[:, a:b]

        def bank(h):
            return slice(HALF * h, HALF * (h + 1))

        def h2_of(c, p):
            return h2[c][p % len(h2[c])]

        def conv_product(engine, seg, oy):
            q = qpad[seg % 2][:]
            taps = w(seg // B, "dw_w").rearrange("p (a k) -> p a k", a=1).broadcast_to([128, WD, KS * KS])\
                .rearrange("p o (a b) -> p o a b", a=KS)
            window = bass.AP(tensor=q.tensor, offset=q.offset + DF * oy * PAD,
                             ap=[q.ap[0], [DF, WD], [PAD, KS], [1, KS]])
            out = conv_prod[:, WD * oy:WD * (oy + 1)].rearrange("p o (a b) -> p o a b", a=KS)
            return engine.tensor_tensor(out, window, taps, ALU.mult)

        def big_free_for_conv(engine, seg):
            if seg >= B:
                engine.wait_ge(x_ready, seg - B + 1)
            elif seg:
                engine.wait_ge(misc_emptied, misc_turn("sample", seg - 1) + 1)

        block = ctx.enter_context(nc.Block())

        @block.sync
        def _(sp):
            def invert_sums(seg):
                sp.wait_ge(misc_emptied, misc_turn("exp_sums", seg) + 1)
                n = packed_sums[:].shape[1]
                den = att_den
                src = bass.AP(tensor=den.tensor, offset=den.offset, ap=[[DH * den.ap[0][0], G], [n, HW // n], [1, n]])
                sp.dma_start(packed_sums[:], src).then_inc(sums_packed, 16)
                sp.wait_ge(reciprocal_ready, seg + 1)
                r = reciprocals_dram[seg]
                sp.dma_start(bass.AP(tensor=r.tensor, offset=r.offset, ap=[[n, 128], [1, n]]), packed_sums[:])\
                    .then_inc(reciprocals_stored, 16)
                sp.wait_ge(reciprocals_stored, 16 * (seg + 1))
                src = bass.AP(tensor=r.tensor, offset=r.offset, ap=[[HW, G], [0, DH], [1, HW]])
                sp.dma_start(att_den, src).then_inc(reciprocals_spread, 16)

            sp.dma_start(x[0][:], x_in[0]).then_inc(x_loaded[0], 16)
            sp.dma_start(wts[0][:, 0:EARLY], weights[0][:, 0:EARLY]).then_inc(early_loaded[0], 16)
            sp.dma_start(const[:], consts).then_inc(const_loaded, 16)
            sp.dma_start(wts[0][:, EARLY:MLP_AT], weights[0][:, EARLY:MLP_AT]).then_inc(late_loaded[0], 16)
            sp.dma_start(x[1][:], x_in[1]).then_inc(x_loaded[1], 16)
            sp.dma_start(wts[1][:, 0:EARLY], weights[1][:, 0:EARLY]).then_inc(early_loaded[1], 16)
            sp.dma_start(wts[1][:, EARLY:MLP_AT], weights[1][:, EARLY:MLP_AT]).then_inc(late_loaded[1], 16)
            sp.dma_start(mlp_wts[:], weights[0][:, MLP_AT:WCOLS]).then_inc(mlp_loaded, 16)
            for unit in range(SEGS * PAIRS):
                seg, pair, p = unit // PAIRS, unit % PAIRS, unit % 2
                if pair == 0:
                    sp.wait_ge(feat_ready, seg + 1)
                    sp.dma_start(features_dram[seg].rearrange("c u k q -> k (c u) q"), feat[:]).then_inc(feat_stored, 16)
                    sp.wait_ge(feat_stored, 16 * (seg + 1))
                    if seg == B + 1:
                        sp.wait_ge(misc_filled, misc_turn("mlp_down", 2 * B - 1) + 1)
                        sp.dma_start(mlp_wts[:], weights[1][:, MLP_AT:WCOLS]).then_inc(mlp_loaded, 16)
                if pair == 2 and seg:
                    invert_sums(seg - 1)
                if unit >= 2:
                    for c in range(CT):
                        sp.wait_ge(sum_ready[c], PARTS[c] * STEPS * (unit - 1))
                for xy, dst in ((0, hx[p]), (1, hy[p])):
                    f = features_dram[seg, xy, pair]
                    for r in range(QUAD):
                        src = bass.AP(tensor=f.tensor, offset=f.offset + STEPS * r * W,
                                      ap=[[0, HID], [4 * STEPS * W, CT], [1, STEPS * W]])
                        sp.dma_start(dst[HID * r:HID * (r + 1)].rearrange("p c t q -> p c (t q)"), src)\
                            .then_inc(feat_loaded[p], 16)
            invert_sums(SEGS - 1)
            sp.wait_ge(x_ready, SEGS - 1)
            sp.dma_start(x_out[0], x[0][:]).then_inc(out_stored, 16)
            for h in range(2):
                sp.wait_ge(x_ready, SEGS + h)
                sp.dma_start(x_out[1][:, bank(h)], x[1][:, bank(h)]).then_inc(out_stored, 16)
            sp.wait_ge(out_stored, 16 * 3)

        @block.gpsimd
        def _(pool):
            def add_terms(p, c, t, g):
                if not (isinstance(g, int) and g == 0):
                    pool.wait_ge(lo_ready[c], g)
                n = ROWS_ON_POOL[c]
                pool.tensor_tensor(h1_sum[c][:, 0:n], hx[p][:, c, t].unsqueeze(1).broadcast_to([128, n, W]),
                                   hy[p][:, c, t, 0:n].unsqueeze(2).broadcast_to([128, n, W]), ALU.add)\
                    .then_inc(sum_ready[c], 1)

            def pick_w3(l, t, g, p):
                if not (isinstance(g, int) and g < 2):
                    pool.wait_ge(bias_added, g - 1)
                pool.tensor_copy(w3_now[p][:], w(l, "w3").rearrange("p (t m) -> p t m", t=STEPS)[:, t])\
                    .then_inc(w3_ready, 1)

            def step(unit_now, t_now, unit_next, t_next, g, p):
                for c in range(CT):
                    add_terms(unit_next % 2, c, t_next, g + 1)
                pick_w3(unit_now // PAIRS // B, t_now, g, p)

            def conv_products(n):
                seg, part = n // 2, n % 2
                pool.wait_ge(q_ready, seg + 1)
                big_free_for_conv(pool, seg)
                for oy in (2 * part, 2 * part + 1):
                    conv_product(pool, seg, oy).then_inc(conv_multiplied[0], 1)

            def hat_products(n):
                seg, part = n // 2, n % 2
                pool.wait_ge(hats_ready, 2 * seg + 1)
                for k in (2 * part, 2 * part + 1):
                    pool.tensor_tensor(bilinear[:, k], hat_y[:, k], hat_x[:], ALU.mult).then_inc(bilinear_ready[0], 1)

            stages = {"conv_products": conv_products, "hat_products": hat_products}
            for p in range(2):
                pool.memset(qpad[p][:], 0.0).then_inc(borders_zeroed, 1)
            pool.wait_ge(early_loaded[0], 16)
            for name, n in PLAN["pool"][-1]:
                stages[name](n)
            pool.wait_ge(terms_ready, 2)
            pool.wait_ge(late_loaded[0], 16)
            for c in range(CT):
                add_terms(0, c, 0, 0)
            for a, pairs in runs("pool", STEPS - 1):
                unit = a // STEPS
                if a % (SEG_STEPS * B) == 0 and a > 0:
                    pool.wait_ge(late_loaded[a // (SEG_STEPS * B)], 16)
                if pairs:
                    with pool.Fori(a, a + 2 * pairs - 1, 2) as g:
                        for k in range(2):
                            t = g + k - STEPS * unit
                            step(unit, t, unit, t + 1, g + k, (a + k) % 2)
                elif a < ALL_STEPS - 1:
                    nxt = a + 1
                    if nxt % STEPS == 0:
                        pool.wait_ge(terms_ready, 2 * (nxt // STEPS + 1))
                    step(unit, a % STEPS, nxt // STEPS, nxt % STEPS, a, a % 2)
                else:
                    pick_w3(unit // PAIRS // B, a % STEPS, a, a % 2)
                for name, n in PLAN["pool"].get(a + max(0, 2 * pairs - 1), []):
                    stages[name](n)

        @block.scalar
        def _(act):
            def relu1(c, g, p):
                act.wait_ge(sum_ready[c], PARTS[c] * (g + 1))
                if not (isinstance(g, int) and g < 2):
                    act.wait_ge(z_ready[c], g - 1)
                act.activation(h1_hi[p][c][:], h1_sum[c][:].rearrange("p y x -> p (y x)"), ACT.Relu)\
                    .then_inc(hi_ready[c], 1)

            def relu2(l, c, g, p):
                if c < 2 and not (isinstance(g, int) and g < 2):
                    act.wait_ge(bias_added, g - 1)
                if c >= 2 and not (isinstance(g, int) and g == 0):
                    act.wait_ge(bias_added, g)
                n = Z_PARTS[c]
                for part in range(n):
                    act.wait_ge(z_ready[c], n * g + (part + 1))
                    s = slice(HW // n * part, HW // n * (part + 1))
                    act.activation(h2_of(c, p)[:, s], z[c % 2][:, s], ACT.Relu, bias=w(l, "b2")).then_inc(h2_ready[c], 1)

            def copy_scores(unit):
                seg = unit // PAIRS
                l = seg // B
                act.wait_ge(bias_added, STEPS * (unit + 1))
                if seg:
                    act.wait_ge(misc_emptied, misc_turn("attend", seg - 1) + 1)
                act.activation(probs[:, unit % PAIRS], scores[:], ACT.Identity, bias=w(l, "b3")).then_inc(scores_copied, 1)

            def step(l, g, p, last=False, copy_of=None):
                if not last:
                    for c in RELU_ON_ACT:
                        relu1(c, g + 1, 1 - p)
                for c in range(CT):
                    relu2(l, c, g, p)
                if copy_of is not None:
                    copy_scores(copy_of)

            def ordered(ins):
                ordered.n += 1
                ins.then_inc(act_order, 1)
                act.wait_ge(act_order, ordered.n)
            ordered.n = 0

            def emptied(ins):
                ins.then_inc(misc_emptied, 1)

            def q_out(seg):
                if seg < 2:
                    act.wait_ge(borders_zeroed, 2)
                act.wait_ge(misc_filled, misc_turn("q", seg) + 1)
                inner = qpad[seg % 2][:, 1:H + 1, 1:W + 1]
                act.activation(inner, misc[:].rearrange("p (y x) -> p y x", y=H), ACT.Copy).then_inc(q_ready, 1)
                act.wait_ge(q_ready, seg + 1)
                act.sem_inc(misc_emptied, 1)

            def image_t_out(seg):
                act.wait_ge(misc_filled, misc_turn("image_t", seg) + 1)
                emptied(act.activation(image_t[:].rearrange("p k c -> p (k c)"), misc[:], ACT.Copy))

            def conv_gelu(seg):
                act.wait_ge(conv_ready, 2 * (seg + 1))
                act.activation(conv_act[:], conv[:], ACT.Gelu, bias=w(seg // B, "dw_b")).then_inc(gelu_ready, 1)

            def offset_tanh(seg):
                act.wait_ge(misc_filled, misc_turn("offset", seg) + 1)
                emptied(act.activation(tanh[:].rearrange("p c u -> p (c u)"), misc[:, 0:2 * PAIRS], ACT.Tanh))

            def features(seg):
                act.wait_ge(pos_ready, seg + 1)
                ordered(act.activation(pos_abs[:], pos[:], ACT.Abs))
                if seg:
                    act.wait_ge(feat_stored, 16 * seg)
                act.activation(pos_sign[:], pos[:], ACT.Sign).then_inc(logs_ready, 1)
                act.activation(pos_log[:], pos_abs[:], ACT.Ln, bias=1.0).then_inc(logs_ready, 1)

            def spread_out(seg):
                act.wait_ge(misc_filled, misc_turn("spread", seg) + 1)
                act.activation(hat_x[:], misc[:, bank(0)], ACT.Abs, bias=cst("neg_x")).then_inc(hats_in, 1)
                act.activation(key_y, misc[:, bank(1)], ACT.Copy).then_inc(hats_in, 1)
                act.wait_ge(hats_in, 2 * (seg + 1))
                act.sem_inc(misc_emptied, 1)

            def distances(n):
                act.wait_ge(hats_in, 2 * (n // 4 + 1))
                act.wait_ge(conv_ready, 2 * (n // 4 + 1))
                for k in (2 * (n % 4), 2 * (n % 4) + 1):
                    act.activation(hat_y[:, k], key_y, ACT.Abs, bias=cst("neg_y")[:, k:k + 1]).then_inc(distances_ready, 1)

            def attention_place_free(seg):
                if seg + 1 < SEGS:
                    act.wait_ge(misc_emptied, misc_turn("sample", seg + 1) + 1)
                else:
                    act.wait_ge(attended_ready, seg)

            def exp_sums_out(seg):
                act.wait_ge(misc_filled, misc_turn("exp_sums", seg) + 1)
                attention_place_free(seg)
                emptied(act.activation(att_den, misc[:], ACT.Copy))

            def attend_out(seg):
                act.wait_ge(misc_filled, misc_turn("attend", seg) + 1)
                attention_place_free(seg)
                emptied(act.activation(att_sum, misc[:], ACT.Copy))

            def keys_values_out(seg):
                act.wait_ge(misc_filled, misc_turn("keys_values", seg) + 1)
                for u in range(PAIRS):
                    rows = slice(32 * u, 32 * (u + 1))
                    ordered(act.activation(keys_t[seg % 2][rows, u], misc[rows, 0:128], ACT.Copy, scale=DH ** -0.5))
                emptied(act.activation(values[seg % 2][:], misc[:, HALF:HALF + C], ACT.Copy))

            def widen_max(unit):
                act.wait_ge(misc_emptied, misc_turn("scores_t", unit) + 1)
                if unit:
                    act.wait_ge(misc_filled, misc_turn("max_spread", unit - 1) + 1)
                act.activation(neg_max_wide[:], neg_max[:].unsqueeze(2).broadcast_to([128, 2 * CHUNKS, NKV]), ACT.Copy)\
                    .then_inc(max_widened, 1)

            def exp(unit):
                act.wait_ge(misc_emptied, misc_turn("max_spread", unit) + 1)
                act.activation(probs[:, unit % PAIRS], probs[:, unit % PAIRS], ACT.Exp).then_inc(exp_ready, 1)

            def mlp_gelu(n):
                seg, c = n // MLP_PARTS, n % MLP_PARTS
                act.wait_ge(misc_filled, misc_turn("mlp_up", n) + 1)
                act.wait_ge(xn2_ready, seg + 1)
                emptied(act.activation(mlp_h[:, c], misc[:], ACT.Gelu, bias=w(seg // B, "mlp_b1")[:, c:c + 1]))

            def tail_gelu(n):
                c = n % MLP_PARTS
                act.wait_ge(tail_up_filled, n + 1)
                if n < MLP_PARTS:
                    act.wait_ge(lo_ready[c], ALL_STEPS)
                else:
                    act.wait_ge(attended_ready, SEGS)
                act.activation(tail_h[n], tail_up_to[n][:], ACT.Gelu, bias=w(LAYERS - 1, "mlp_b1")[:, c:c + 1])\
                    .then_inc(tail_gelu_done, 1)

            stages = {"q_out": q_out, "image_t_out": image_t_out, "conv_gelu": conv_gelu,
                      "offset_tanh": offset_tanh, "features": features, "spread_out": spread_out,
                      "distances": distances, "attend_out": attend_out, "exp_sums_out": exp_sums_out,
                      "keys_values_out": keys_values_out, "exp": exp, "widen_max": widen_max,
                      "mlp_gelu": mlp_gelu, "tail_gelu": tail_gelu}
            act.wait_ge(setup_done, 1)
            ordered(act.activation(conv_act[:, 0:1], keys_t[0][:, 0, 0:1], ACT.Gelu))
            act.wait_ge(const_loaded, 16)
            act.wait_ge(early_loaded[0], 16)
            for name, n in PLAN["act"][-1]:
                stages[name](n)
            act.wait_ge(late_loaded[0], 16)
            for c in RELU_ON_ACT:
                relu1(c, 0, 0)
            for a, pairs in runs("act", 0):
                l = a // (SEG_STEPS * B)
                if a == SEG_STEPS - STEPS:
                    act.wait_ge(early_loaded[1], 16)
                if pairs:
                    with act.Fori(a, a + 2 * pairs - 1, 2) as g:
                        for k in range(2):
                            step(l, g + k, (a + k) % 2)
                else:
                    copy_of = a // STEPS - 1 if a % STEPS == 0 and a > 0 else None
                    step(l, a, a % 2, last=a == ALL_STEPS - 1, copy_of=copy_of)
                for name, n in PLAN["act"].get(a + max(0, 2 * pairs - 1), []):
                    stages[name](n)
            copy_scores(SEGS * PAIRS - 1)
            for g in range(ALL_STEPS, max(PLAN["act"]) + 1):
                for name, n in PLAN["act"].get(g, []):
                    stages[name](n)

        @block.vector
        def _(dve):
            def ordered(ins):
                ordered.n += 1
                ins.then_inc(dve_order, 1)
                dve.wait_ge(dve_order, ordered.n)
            ordered.n = 0

            def add_terms(u, c, t, g):
                if not (isinstance(g, int) and g == 0):
                    dve.wait_ge(lo_ready[c], g)
                a = ROWS_ON_POOL[c]
                dve.tensor_tensor(h1_sum[c][:, a:H], hx[u][:, c, t].unsqueeze(1).broadcast_to([128, H - a, W]),
                                  hy[u][:, c, t, a:H].unsqueeze(2).broadcast_to([128, H - a, W]), ALU.add)\
                    .then_inc(sum_ready[c], 1)

            def first_layer(c, g, p):
                total = h1_sum[c][:].rearrange("p y x -> p (y x)")
                if not (isinstance(g, int) and g < 2):
                    dve.wait_ge(z_ready[c], Z_PARTS[c] * (g - 1))
                if c not in RELU_ON_ACT:
                    dve.wait_ge(sum_ready[c], PARTS[c] * (g + 1))
                    dve.tensor_scalar(h1_hi[p][c][:], total, 0.0, None, ALU.max).then_inc(hi_ready[c], 1)
                dve.wait_ge(hi_ready[c], g + 1)
                dve.scalar_tensor_tensor(out=h1_lo[p][c][:], in0=total, scalar=0.0, in1=h1_hi[p][c][:].bitcast(F32),
                                         op0=ALU.max, op1=ALU.subtract).then_inc(lo_ready[c], 1)

            def step(u, t, g, p):
                for c in range(CT):
                    if ROWS_ON_POOL[c] < H:
                        add_terms(u, c, t, g)
                for c in range(CT):
                    first_layer(c, g, p)

            def norm1(seg):
                l, b = seg // B, seg % B
                if seg < B:
                    dve.wait_ge(x_loaded[b], 16)
                else:
                    dve.wait_ge(x_ready, seg - B + 1)
                if seg >= B:
                    dve.wait_ge(misc_emptied, misc_turn("mlp_down", 2 * (seg - B) + 1) + 1)
                elif seg:
                    dve.wait_ge(distances_ready, CHUNKS * seg)
                dve.tensor_scalar(xn[:], x[b][:], scale[:, l, 0:1], w(l, "bn1_b"), ALU.mult, ALU.add)\
                    .then_inc(xn_ready, 1)

            def conv_products(n):
                seg, part = n // 2, n % 2
                dve.wait_ge(q_ready, seg + 1)
                big_free_for_conv(dve, seg)
                for oy in (HD // 2 + 2 * part, HD // 2 + 2 * part + 1):
                    conv_product(dve, seg, oy).then_inc(conv_multiplied[1], 1)

            def conv_sum(n):
                seg, part = n // 2, n % 2
                dve.wait_ge(conv_multiplied[part], HD // 2 * (seg + 1))
                if seg >= 1:
                    dve.wait_ge(gelu_ready, seg)
                s = slice(NKV // 2 * part, NKV // 2 * (part + 1))
                dve.tensor_reduce(conv[:, s], conv_prod[:, s], AX_X, ALU.add).then_inc(conv_ready, 1)

            def positions(seg):
                dve.wait_ge(misc_emptied, misc_turn("offset", seg) + 1)
                if seg >= 1:
                    dve.wait_ge(misc_emptied, misc_turn("spread", seg - 1) + 1)
                    dve.wait_ge(logs_ready, 2 * seg)
                for xy in range(2):
                    ordered(dve.tensor_scalar(coord[:, 0, PAIRS * xy:PAIRS * (xy + 1)], tanh[:, xy], OFF_SCALE,
                                              cst("gridkv")[:, xy:xy + 1], ALU.mult, ALU.add))
                ordered(dve.tensor_scalar(coord[:, 1], coord[:, 0], 2.0, 1.0 / (HD - 1), ALU.mult, ALU.mult))
                ordered(dve.tensor_scalar(coord[:, 2], coord[:, 1], -1.0, None, ALU.add))
                ordered(dve.tensor_scalar(coord[:, 1], coord[:, 2], 1.0, W / 2.0, ALU.add, ALU.mult))
                ordered(dve.tensor_scalar(coord[:, 3], coord[:, 1], -0.5, None, ALU.add))
                dve.tensor_tensor(pos[:], cst("gridq").unsqueeze(1).broadcast_to([128, 2 * PAIRS, W]),
                                  coord[:, 2].unsqueeze(2).broadcast_to([128, 2 * PAIRS, W]), ALU.subtract)\
                    .then_inc(pos_ready, 1)

            def features_sign(seg):
                dve.wait_ge(logs_ready, 2 * (seg + 1))
                dve.tensor_tensor(feat[:], pos_sign[:], pos_log[:], ALU.mult).then_inc(feat_ready, 1)

            def hats(n):
                dve.wait_ge(distances_ready, CHUNKS // 2 * (n + 1))
                if n % 2 == 0:
                    dve.tensor_scalar(hat_x[:], hat_x[:], 1.0, 1.0, ALU.min, ALU.subtract).then_inc(hat_x_ready, 1)
                    dve.wait_ge(hat_x_ready, n // 2 + 1)
                y = hat_y[:, 4 * (n % 2):4 * (n % 2) + 4]
                dve.tensor_scalar(y, y, 1.0, 1.0, ALU.min, ALU.subtract).then_inc(hats_ready, 1)

            def hat_products(n):
                seg, part = n // 2, n % 2
                dve.wait_ge(hats_ready, 2 * seg + 2)
                for k in (CHUNKS // 2 + 2 * part, CHUNKS // 2 + 2 * part + 1):
                    dve.tensor_tensor(bilinear[:, k], hat_y[:, k], hat_x[:], ALU.mult).then_inc(bilinear_ready[1], 1)

            def sample_out(seg):
                dve.wait_ge(misc_filled, misc_turn("sample", seg) + 1)
                if seg >= 1:
                    dve.wait_ge(misc_emptied, misc_turn("keys_values", seg - 1) + 1)
                dve.tensor_tensor(sampled[:], misc[:, 0:128].rearrange("p (h k) -> p h k", h=2),
                                  cst("own").unsqueeze(2).broadcast_to([128, 2, NKV]), ALU.mult)\
                    .then_inc(misc_emptied, 1)

            def hidden_terms(n):
                unit, xy = n // 2, n % 2
                l, p = unit // PAIRS // B, unit % 2
                dve.wait_ge(feat_loaded[p], 16 * 2 * QUAD * (unit // 2 + 1))
                if xy == 0:
                    dve.tensor_scalar(hx[p][:], hx[p][:], w(l, "w1x"), None, ALU.mult).then_inc(terms_ready, 1)
                else:
                    dve.tensor_scalar(hy[p][:], hy[p][:], w(l, "w1y"), w(l, "b1"), ALU.mult, ALU.add)\
                        .then_inc(terms_ready, 1)

            def score_max(unit):
                dve.wait_ge(misc_filled, misc_turn("scores_t", unit) + 1)
                if unit:
                    dve.wait_ge(max_widened, unit)
                dve.tensor_reduce(neg_max[:],
                                  misc[:].rearrange("p (n j) -> p n j", j=NKV), AX_X, ALU.max, negate=True)\
                    .then_inc(misc_emptied, 1)

            def max_off(unit):
                dve.wait_ge(misc_filled, misc_turn("max_spread", unit) + 1)
                s = probs[:, unit % PAIRS]
                dve.tensor_tensor(s, s, misc[:], ALU.add).then_inc(misc_emptied, 1)

            def reciprocal(seg):
                dve.wait_ge(sums_packed, 16 * (seg + 1))
                dve.reciprocal(packed_sums[:], packed_sums[:]).then_inc(reciprocal_ready, 1)

            def divide(seg):
                dve.wait_ge(reciprocals_spread, 16 * (seg + 1))
                dve.wait_ge(misc_emptied, misc_turn("attend", seg) + 1)
                if seg + 1 < SEGS:
                    dve.wait_ge(distances_ready, CHUNKS * (seg + 2))
                else:
                    dve.wait_ge(tail_up_filled, MLP_PARTS)
                dve.tensor_tensor(attended[:], att_sum, att_den, ALU.mult).then_inc(attended_ready, 1)

            def residual1(seg):
                l, b = seg // B, seg % B
                dve.wait_ge(misc_filled, misc_turn("project", seg) + 1)
                dve.scalar_tensor_tensor(out=x[b][:], in0=misc[:], scalar=w(l, "out_b"), in1=x[b][:],
                                         op0=ALU.add, op1=ALU.add).then_inc(misc_emptied, 1)
                dve.wait_ge(misc_emptied, misc_turn("project", seg) + 1)
                dve.tensor_scalar(xn2[:], x[b][:], scale[:, l, 1:2], w(l, "bn2_b"), ALU.mult, ALU.add)\
                    .then_inc(xn2_ready, 1)

            def residual2(n):
                seg, h = n // 2, n % 2
                dve.wait_ge(misc_filled, misc_turn("mlp_down", n) + 1)
                add_mlp(seg, bank(h), misc).then_inc(misc_emptied, 1)
                if h == 1:
                    dve.wait_ge(misc_emptied, misc_turn("mlp_down", n) + 1)
                    dve.sem_inc(x_ready, 1)

            def tail_residual2(n):
                dve.wait_ge(tail_down_filled, n + 1)
                if n == 0:
                    add_mlp(TAIL_SEG, slice(0, HW), tail_down_to[0]).then_inc(x_ready, 1)
                else:
                    add_mlp(SEGS - 1, bank(n - 1), tail_down_to[1]).then_inc(x_ready, 1)

            def add_mlp(seg, s, added):
                b = seg % B
                return dve.scalar_tensor_tensor(out=x[b][:, s], in0=added[:, s], scalar=w(seg // B, "mlp_b2"), in1=x[b][:, s],
                                                op0=ALU.add, op1=ALU.add)

            def set_up(l):
                dve.wait_ge(early_loaded[l], 16)
                for k, name in ((0, "bn1_g"), (1, "bn2_g")):
                    ordered(dve.tensor_scalar(scale[:, l, k:k + 1], w(l, name), float(1.0 / np.sqrt(1.0 + EPS)), None,
                                              ALU.mult))

            def split_w2(l):
                dve.wait_ge(late_loaded[l], 16)
                ordered(dve.tensor_copy(w2_hi[l][:], w(l, "w2")))
                ordered(dve.tensor_tensor(w2_lo[l][:], w(l, "w2"), w2_hi[l][:].bitcast(F32), ALU.subtract))

            stages = {"norm1": norm1, "conv_sum": conv_sum, "positions": positions,
                      "features_sign": features_sign, "hats": hats, "conv_products": conv_products,
                      "hat_products": hat_products, "sample_out": sample_out, "hidden_terms": hidden_terms,
                      "score_max": score_max, "max_off": max_off, "divide": divide, "reciprocal": reciprocal,
                      "residual1": residual1, "residual2": residual2, "tail_residual2": tail_residual2}
            ordered(dve.memset(keys_t[0][:], 0.0))
            dve.memset(keys_t[1][:], 0.0).then_inc(setup_done, 1)
            dve.wait_ge(const_loaded, 16)
            ordered(dve.tensor_copy(ident_r[:], cst("ident")))
            set_up(0)
            for name, n in PLAN["dve"][-1]:
                stages[name](n)
                if name == "features_sign":
                    for l in range(LAYERS):
                        split_w2(l)
                    set_up(1)
                    dve.sem_inc(setup_done, 1)
            dve.wait_ge(terms_ready, 2)
            step(0, 0, 0, 0)
            for name, n in PLAN["dve"][-0.5]:
                stages[name](n)
            for a, pairs in runs("dve", STEPS - 1):
                unit = a // STEPS
                if pairs:
                    with dve.Fori(a, a + 2 * pairs - 1, 2) as g:
                        for k in range(2):
                            step(unit % 2, g + (k + 1 - STEPS * unit), g + (k + 1), (a + k + 1) % 2)
                elif a < ALL_STEPS - 1:
                    if (a + 1) % STEPS == 0:
                        dve.wait_ge(terms_ready, 2 * ((a + 1) // STEPS + 1))
                    step((a + 1) // STEPS % 2, (a + 1) % STEPS, a + 1, (a + 1) % 2)
                for name, n in PLAN["dve"].get(a + max(0, 2 * pairs - 1), []):
                    stages[name](n)
            for g in range(ALL_STEPS, max(PLAN["dve"]) + 1):
                for name, n in PLAN["dve"].get(g, []):
                    stages[name](n)

        @block.tensor
        def _(pe):
            def layer2(l, c, g, p):
                pe.wait_ge(lo_ready[c], g + 1)
                pe.wait_ge(hi_ready[c], g + 1)
                n, before = Z_PARTS[c], (c + 2) % CT
                for h in range(2):
                    out = z[c % 2][:, bank(h)]
                    if c >= 2 and h == 0:
                        pe.wait_ge(h2_ready[before], g + 1)
                    elif c < 2 and not (isinstance(g, int) and g == 0):
                        pe.wait_ge(h2_ready[before], 2 * g + (h - 1))
                    pe.matmul(out, w2_hi[l][:], h1_hi[p][c][:, bank(h)], start=True, stop=False)
                    pe.matmul(out, w2_hi[l][:], h1_lo[p][c][:, bank(h)], start=False, stop=False)
                    ins = pe.matmul(out, w2_lo[l][:], h1_hi[p][c][:, bank(h)], start=False, stop=True)
                    if h == 1 or n == 2:
                        ins.then_inc(z_ready[c], 1)

            def layer3(g, p, last):
                pe.wait_ge(w3_ready, g + 1)
                for c in range(CT):
                    pe.wait_ge(h2_ready[c], Z_PARTS[c] * (g + 1))
                for h in range(2):
                    for c in range(CT):
                        ins = pe.matmul(scores[32 * c:32 * (c + 1), bank(h)], w3_now[p][:], h2_of(c, p)[:, bank(h)],
                                        start=False, stop=last, skip_group_check=True)
                ins.then_inc(bias_added, 1)

            def step(l, g, p):
                static = isinstance(g, int)
                for c in range(CT):
                    layer2(l, c, g, p)
                    if c == 1 and not (static and g == 0):
                        if static and g % STEPS == 1:
                            scores_start(g // STEPS)
                        layer3(g - 1, 1 - p, static and g % STEPS == 0)

            def turn(stage, n):
                k = misc_turn(stage, n)
                if k:
                    pe.wait_ge(misc_emptied, k)

            def filled(ins):
                ins.then_inc(misc_filled, 1)

            def q(seg):
                pe.wait_ge(xn_ready, seg + 1)
                turn("q", seg)
                for h in range(2):
                    ins = pe.matmul(misc[:, bank(h)], w(seg // B, "qw"), xn[:, bank(h)], start=True, stop=True)
                filled(ins)

            def image_transpose(seg):
                turn("image_t", seg)
                for k in range(CHUNKS):
                    s = slice(128 * k, 128 * (k + 1))
                    ins = pe.transpose(misc[:, s], xn[:, s], cst("ident"))
                filled(ins)

            def offset(seg):
                pe.wait_ge(gelu_ready, seg + 1)
                turn("offset", seg)
                pw = w(seg // B, "pw").rearrange("p (h n) -> p h n", h=2)
                for h in range(2):
                    ins = pe.matmul(misc[NKV * h:NKV * (h + 1), 0:2 * PAIRS], conv_act[:], pw[:, h], start=True, stop=True)
                filled(ins)

            def spread(seg):
                pe.wait_ge(pos_ready, seg + 1)
                turn("spread", seg)
                for n in range(2 * PAIRS):
                    ins = pe.matmul(misc[:, 128 * n:128 * (n + 1)], coord[:, 3, n:n + 1].broadcast_to([128, 128]),
                                    cst("ident"), start=True, stop=True)
                filled(ins)

            def sample(seg):
                for k in range(2):
                    pe.wait_ge(bilinear_ready[k], 4 * (seg + 1))
                turn("sample", seg)
                for k in range(CHUNKS):
                    for u in range(PAIRS):
                        ins = pe.matmul(misc[32 * u:32 * (u + 1), 0:128], image_t[:, k, 32 * u:32 * (u + 1)],
                                        bilinear[:, k, 128 * u:128 * (u + 1)], start=k == 0, stop=k == CHUNKS - 1)
                filled(ins)

            def keys_values(seg):
                turn("keys_values", seg)
                s = sampled[:].rearrange("p h k -> p (h k)")
                pe.matmul(misc[:, 0:128], w(seg // B, "kw"), s, start=True, stop=True)
                filled(pe.matmul(misc[:, HALF:HALF + C], s, w(seg // B, "vw"), start=True, stop=True))

            def scores_start(unit):
                seg, u = unit // PAIRS, unit % PAIRS
                if unit:
                    pe.wait_ge(scores_copied, unit)
                pe.wait_ge(misc_emptied, misc_turn("keys_values", seg) + 1)
                for h in range(2):
                    pe.matmul(scores[:, bank(h)], keys_t[seg % 2][:, u], qpad[seg % 2][:, 1 + H // 2 * h:1 + H // 2 * (h + 1), 1:W + 1],
                              start=True, stop=False, skip_group_check=True)

            def scores_transpose(unit):
                pe.wait_ge(scores_copied, unit + 1)
                turn("scores_t", unit)
                for k in range(CHUNKS):
                    s = slice(128 * k, 128 * (k + 1))
                    ins = pe.transpose(misc[:, s], probs[:, unit % PAIRS, s], cst("ident"))
                filled(ins)

            def max_spread(unit):
                turn("max_spread", unit)
                pe.wait_ge(max_widened, unit + 1)
                for k in range(CHUNKS):
                    ins = pe.matmul(misc[:, 128 * k:128 * (k + 1)],
                                    neg_max_wide[:, 2 * k:2 * (k + 1)].rearrange("p n j -> p (n j)"),
                                    ident_r[:], start=True, stop=True)
                filled(ins)

            def over_keys(seg, keys_to_channels):
                pe.wait_ge(exp_ready, PAIRS * (seg + 1))
                for h in range(2):
                    for u in range(PAIRS):
                        ins = pe.matmul(misc[32 * u:32 * (u + 1), bank(h)], keys_to_channels(u), probs[:, u, bank(h)],
                                        start=True, stop=True)
                filled(ins)

            def exp_sums(seg):
                turn("exp_sums", seg)
                over_keys(seg, lambda u: cst("ones"))

            def attend(seg):
                turn("attend", seg)
                over_keys(seg, lambda u: values[seg % 2][:, 32 * u:32 * (u + 1)])

            def project(seg):
                pe.wait_ge(attended_ready, seg + 1)
                turn("project", seg)
                for h in range(2):
                    ins = pe.matmul(misc[:, bank(h)], w(seg // B, "out_w"), attended[:, bank(h)], start=True, stop=True)
                filled(ins)

            def mlp_up(n):
                seg, c = n // MLP_PARTS, n % MLP_PARTS
                pe.wait_ge(mlp_loaded, 16 * (seg // B + 1))
                pe.wait_ge(xn2_ready, seg + 1)
                turn("mlp_up", n)
                for h in range(2):
                    ins = pe.matmul(misc[:, bank(h)], w(seg // B, "mlp_w1")[:, 128 * c:128 * (c + 1)], xn2[:, bank(h)],
                                    start=True, stop=True)
                filled(ins)

            def mlp_down(n):
                seg, h = n // 2, n % 2
                turn("mlp_down", n)
                for c in range(MLP_PARTS):
                    ins = pe.matmul(misc[:, bank(h)], w(seg // B, "mlp_w2")[:, 128 * c:128 * (c + 1)], mlp_h[:, c, bank(h)],
                                    start=c == 0, stop=c == MLP_PARTS - 1)
                filled(ins)

            def tail_up(n):
                seg, c = TAIL_SEG + n // MLP_PARTS, n % MLP_PARTS
                pe.wait_ge(mlp_loaded, 16 * LAYERS)
                pe.wait_ge(xn2_ready, seg + 1)
                if tail_up_to[n] is scores:
                    pe.wait_ge(x_ready, SEGS - 1)
                elif n in (2, 3, 4, 5):
                    pe.wait_ge(tail_gelu_done, n - 1)
                elif tail_up_to[n] is misc:
                    pe.wait_ge(misc_emptied, misc_turn("project", SEGS - 1) + 1)
                for h in range(2):
                    ins = pe.matmul(tail_up_to[n][:, bank(h)], w(LAYERS - 1, "mlp_w1")[:, 128 * c:128 * (c + 1)],
                                    xn2[:, bank(h)], start=True, stop=True)
                ins.then_inc(tail_up_filled, 1)

            def tail_down(n):
                c, to = n % MLP_PARTS, tail_down_to[n // MLP_PARTS]
                if n == 0:
                    pe.wait_ge(scores_copied, SEGS * PAIRS)
                pe.wait_ge(tail_gelu_done, n + 1)
                for h in range(2):
                    ins = pe.matmul(to[:, bank(h)], w(LAYERS - 1, "mlp_w2")[:, 128 * c:128 * (c + 1)],
                                    tail_h[n][:, bank(h)], start=c == 0, stop=c == MLP_PARTS - 1)
                    if n == 2 * MLP_PARTS - 1 or n == MLP_PARTS - 1 and h == 1:
                        ins.then_inc(tail_down_filled, 1)

            stages = {"q": q, "image_t": image_transpose, "offset": offset, "spread": spread, "sample": sample,
                      "keys_values": keys_values, "scores_t": scores_transpose, "max_spread": max_spread,
                      "attend": attend, "exp_sums": exp_sums, "tail_up": tail_up, "tail_down": tail_down,
                      "project": project, "mlp_up": mlp_up, "mlp_down": mlp_down}
            pe.wait_ge(const_loaded, 16)
            pe.wait_ge(early_loaded[0], 16)
            for name, n in PLAN["pe"][-1]:
                stages[name](n)
            pe.wait_ge(late_loaded[0], 16)
            pe.wait_ge(setup_done, 2)
            for a, pairs in runs("pe", 1):
                l = a // (SEG_STEPS * B)
                if a == SEG_STEPS - STEPS:
                    pe.wait_ge(early_loaded[1], 16)
                    pe.wait_ge(late_loaded[1], 16)
                if pairs:
                    with pe.Fori(a, a + 2 * pairs - 1, 2) as g:
                        for k in range(2):
                            step(l, g + k, (a + k) % 2)
                else:
                    step(l, a, a % 2)
                for name, n in PLAN["pe"].get(a + max(0, 2 * pairs - 1), []):
                    stages[name](n)
            layer3(ALL_STEPS - 1, (ALL_STEPS - 1) % 2, True)
            for g in range(ALL_STEPS, max(PLAN["pe"]) + 1):
                for name, n in PLAN["pe"].get(g, []):
                    stages[name](n)


def lay_out_weights(get):
    out = np.zeros((128, WCOLS), np.float32)

    def put(name, a):
        lo, hi = COLS[name]
        out[:, lo:hi] = np.reshape(a, (128, hi - lo))

    for name in ("bn1_g", "bn1_b", "bn2_g", "bn2_b", "out_b", "mlp_b2"):
        put(name, get(name))
    put("dw_b", np.tile(get("off_dw_b"), G))
    put("w1x", np.tile(get("cpb_w1")[0], QUAD))
    put("w1y", np.tile(get("cpb_w1")[1], QUAD))
    put("b1", np.tile(get("cpb_b1"), QUAD))
    put("b2", np.tile(get("cpb_b2"), QUAD))
    put("b3", np.tile(get("cpb_b3"), 128))
    put("mlp_b1", get("mlp_b1").reshape(MLP_PARTS, 128).T)
    put("dw_w", np.tile(get("off_dw_w").reshape(DH, KS * KS), (G, 1)))
    pw = np.zeros((G, DH, 2, 2, PAIRS), np.float32)
    for g in range(G):
        pw[g, :, g % 2, :, g // 2] = get("off_pw_w").T
    put("pw", pw)
    for name, key in (("qw", "qw"), ("kw", "kw"), ("vw", "vw")):
        a = np.zeros((G, DH, G, DH), np.float32)
        for g in range(G):
            a[g, :, g, :] = get(key)[g].T
        put(name, a)
    put("out_w", get("out_w").T)
    w2 = np.zeros((QUAD, HID, QUAD, HID), np.float32)
    w3 = np.zeros((QUAD, HID, STEPS, 32), np.float32)
    for r in range(QUAD):
        w2[r, :, r, :] = get("cpb_w2")
        for t in range(STEPS):
            w3[r, :, t, STEPS * r + t] = get("cpb_w3")[:, 0]
    put("w2", w2)
    put("w3", w3)
    put("mlp_w1", get("mlp_w1").T)
    put("mlp_w2", get("mlp_w2").reshape(C, MLP_PARTS, 128).transpose(2, 1, 0))
    return out


def constants():
    out = np.zeros((128, CCOLS), np.float32)
    p = np.arange(128)

    def put(name, a):
        lo, hi = CONST[name]
        out[:, lo:hi] = a

    put("ident", np.eye(128))
    grid = (np.float32(2.0) * np.arange(W, dtype=np.float32) / np.float32(W - 1) - np.float32(1.0)).astype(np.float32)
    put("gridq", np.broadcast_to(grid, (128, W)))
    put("gridkv", np.stack([p % NKV % WD, p % NKV // WD], 1))
    put("neg_x", -(p % W)[:, None])
    put("neg_y", -4 * np.arange(CHUNKS)[None, :] - (p // W)[:, None])
    put("ones", p[:, None] // NKV == np.arange(32)[None, :] // DH)
    put("own", (p // DH % 2)[:, None] == np.arange(2)[None, :])
    return out


def kernel(**inputs):
    import concourse.bacc as bacc
    from concourse.bass_utils import run_bass_kernel_spmd

    nc = bacc.Bacc("TRN2", target_bir_lowering=False, num_devices=1)
    weights = np.zeros((LAYERS, 128, WCOLS), np.float32)
    for l in range(LAYERS):
        weights[l] = lay_out_weights(lambda name: np.asarray(inputs[f"L{l}_conv_{name}"]))
    arrays = {"x_dram": np.ascontiguousarray(np.asarray(inputs["x"]).reshape(B, C, HW)),
              "consts_dram": constants(), "weights_dram": weights}
    args = [nc.dram_tensor(n, a.shape, F32, kind="ExternalInput").ap() for n, a in arrays.items()]
    out = nc.dram_tensor("out_dram", (B, C, HW), F32, kind="ExternalOutput").ap()
    features = nc.dram_tensor("features_dram", (SEGS, 2, PAIRS, 2 * NKV, W), F32, kind="Internal").ap()
    reciprocals = nc.dram_tensor("reciprocals_dram", (SEGS, G, HW), F32, kind="Internal").ap()
    build(nc, *args, out, features, reciprocals)
    r = run_bass_kernel_spmd(nc, [arrays], core_ids=[0])
    return r.results[0]["out_dram"].reshape(B, C, H, W)
```
